# Optimizing a Trainium2 kernel written in Bass

```python
import numpy as np
import jax
import jax.numpy as jnp

def _softmax(x, axis=-1):
    return jax.nn.softmax(x, axis=axis)

def _gelu(x):
    return jax.nn.gelu(x, approximate=True)

def _silu(x):
    return jax.nn.silu(x)

def _sigmoid(x):
    return jax.nn.sigmoid(x)

def _layernorm(x, axis=-1, eps=1e-05):
    m = jnp.mean(x, axis=axis, keepdims=True)
    v = jnp.var(x, axis=axis, keepdims=True)
    return (x - m) / jnp.sqrt(v + eps)

def _scatter_add(tgt, idx, src, axis=0):
    return tgt.at[idx].add(src)

def _segment_sum(src, seg, n):
    return jax.ops.segment_sum(src, seg, n)
kernel_name = 'mk_prb_d1_jaxref_r2_00b38e'

def setup_inputs(seed: int=0):
    np.random.seed(seed)
    _w = jnp.asarray

    def _L0_attn_setup():
        import jax, jax.numpy as jnp
        import numpy as np
        DIM = 512
        NUM_HEADS = 16
        HEAD_DIM = DIM // NUM_HEADS
        SCALE = HEAD_DIM ** (-0.5)
        key = jax.random.key(seed)
        k1, k2, k3 = jax.random.split(key, 3)
        B, N, C = (4, 2048, DIM)
        x = jax.random.normal(k1, (B, N, C), dtype=jnp.float32)
        W_qkv = jax.random.normal(k2, (C, 3 * C), dtype=jnp.float32) * C ** (-0.5)
        b_qkv = jax.random.normal(k3, (3 * C,), dtype=jnp.float32) * 0.01
        return {'x': x, 'W_qkv': W_qkv, 'b_qkv': b_qkv}
    _L0_attn_in = _L0_attn_setup()

    def _L0_ffn_setup():
        import jax, jax.numpy as jnp
        import numpy as np
        EPS = 1e-08

        def _ternary_linear(x, w):
            alpha = jnp.mean(jnp.abs(w))
            w_t = jnp.sign(w) * (jnp.abs(w) > 0.5 * alpha).astype(w.dtype)
            w_q = w + jax.lax.stop_gradient(w_t - w)
            d = x.shape[-1]
            rms = jnp.sqrt(jnp.sum(x * x, axis=-1, keepdims=True)) / jnp.sqrt(jnp.asarray(d, x.dtype))
            x_norm = x / (rms + EPS)
            return jnp.einsum('bsd,fd->bsf', x_norm, w_q)
        key = jax.random.key(seed)
        k1, k2, k3 = jax.random.split(key, 3)
        d_model, d_ff = (512, 2048)
        B, S = (4, 2048)
        x = jax.random.normal(k1, (B, S, d_model), dtype=jnp.float32)
        w_up = jax.random.normal(k2, (d_ff, d_model), dtype=jnp.float32) * 0.02
        w_down = jax.random.normal(k3, (d_model, d_ff), dtype=jnp.float32) * 0.02
        return {'x': x, 'w_up': w_up, 'w_down': w_down}
    _L0_ffn_in = _L0_ffn_setup()
    _d = {'L0_attn_x': _L0_attn_in['x'], 'L0_attn_W_qkv': _L0_attn_in['W_qkv'], 'L0_attn_b_qkv': _L0_attn_in['b_qkv'], 'L0_ffn_w_up': _L0_ffn_in['w_up'], 'L0_ffn_w_down': _L0_ffn_in['w_down']}
    _x0 = _d['L0_attn_x']
    _d['L0_attn_x'] = jax.random.normal(jax.random.fold_in(jax.random.key(seed), 1), (8, 1024, 512), dtype=_x0.dtype)
    del _x0
    return _d

def reference(L0_attn_x, L0_attn_W_qkv, L0_attn_b_qkv, L0_ffn_w_up, L0_ffn_w_down):

    def _L0_attn_ref(x, W_qkv, b_qkv):
        import jax, jax.numpy as jnp
        import numpy as np
        DIM = 512
        NUM_HEADS = 16
        HEAD_DIM = DIM // NUM_HEADS
        SCALE = HEAD_DIM ** (-0.5)
        B, N, C = x.shape
        H, D = (NUM_HEADS, HEAD_DIM)
        qkv = x @ W_qkv + b_qkv
        qkv = qkv.reshape(B, N, 3, H, D)
        q, k, v = (qkv[:, :, 0], qkv[:, :, 1], qkv[:, :, 2])
        q = q * SCALE
        k = jax.nn.softmax(k, axis=-1)
        attn = jnp.einsum('bnhd,bngd->bnhg', q, k)
        out = jnp.einsum('bnhg,bngd->bnhd', attn, v)
        return out.reshape(B, N, C)

    def _L0_ffn_ref(x, w_up, w_down):
        import jax, jax.numpy as jnp
        import numpy as np
        EPS = 1e-08

        def _ternary_linear(x, w):
            alpha = jnp.mean(jnp.abs(w))
            w_t = jnp.sign(w) * (jnp.abs(w) > 0.5 * alpha).astype(w.dtype)
            w_q = w + jax.lax.stop_gradient(w_t - w)
            d = x.shape[-1]
            rms = jnp.sqrt(jnp.sum(x * x, axis=-1, keepdims=True)) / jnp.sqrt(jnp.asarray(d, x.dtype))
            x_norm = x / (rms + EPS)
            return jnp.einsum('bsd,fd->bsf', x_norm, w_q)
        h = jax.nn.gelu(_ternary_linear(x, w_up), approximate=False)
        return _ternary_linear(h, w_down)
    x = L0_attn_x
    xn = _layernorm(x, axis=-1)
    x = x + _L0_attn_ref(xn, L0_attn_W_qkv, L0_attn_b_qkv) + _L0_ffn_ref(xn, L0_ffn_w_up, L0_ffn_w_down)
    return x

_drawn_inputs = setup_inputs


def setup_inputs(seed=0):
    import zlib

    import numpy as np

    out = dict(_drawn_inputs(seed))
    spreads = {}
    factors = {'L0_attn_W_qkv': 8.0, 'L0_attn_b_qkv': 8.0}
    for name, (base, spread) in spreads.items():
        noise = np.random.default_rng([zlib.crc32(name.encode()), seed]).standard_normal(out[name].shape)
        drawn = base * np.exp(spread * noise) if base else spread * noise
        out[name] = jnp.asarray(drawn.astype(out[name].dtype))
    for name, factor in factors.items():
        out[name] = (out[name] * factor).astype(out[name].dtype)
    return out
```

```python
from contextlib import ExitStack

import numpy as np

import concourse.bass as bass
from concourse import mybir

ALU = mybir.AluOpType
ACT = mybir.ActivationFunctionType
AX = mybir.AxisListType
F32 = mybir.dt.float32
F16 = mybir.dt.float16
U32 = mybir.dt.uint32

P = 128
HEADS = 16
X_SCALE = 2.0 ** 10
H_SCALE = 2.0 ** 6
K_SCALE = 2.0 ** 14
TOP = 2.0 ** 14
LN_EPS = 1e-5
RMS_EPS = 1e-8
TINY = 1e-30


def carve(region, sizes):
    out, at = {}, 0
    for name, (shape, dt) in sizes.items():
        words = int(np.prod(shape)) * (2 if dt == F16 else 4) // 4
        v = region[:, at:at + words]
        if dt != F32:
            v = v.bitcast(dt)
        if len(shape) == 2:
            v = v.rearrange("p (a b) -> p a b", a=shape[0])
        if len(shape) == 3:
            v = v.rearrange("p (a b c) -> p a b c", a=shape[0], b=shape[1])
        out[name] = v
        at += words
    assert at <= region.shape[1], (at, region.shape)
    return out


def layer_kernel(nc, x, w_qkv, b_qkv, w_up, w_down, out):
    batch, seq, C = x.shape
    TOKENS = batch * seq
    FF = w_up.shape[0]
    D = C // HEADS
    SCALE = float(D) ** -0.5
    TILES = 4
    GT = TILES * P
    GROUPS = TOKENS // GT
    CC = C // P
    FC = FF // P
    PAIRS = FC // 2
    OCT = P // 8
    assert C == 512 and D == 32 and FC == 16 and CC == 4

    x_groups = x.rearrange("a b c -> (a b) c").rearrange("(s i p) c -> s p i c", i=TILES, p=P)
    out_tiles = out.rearrange("a b c -> (a b) c").rearrange("(s i p) c -> s i p c", i=TILES, p=P)

    with ExitStack() as ctx:
        def sb(name, shape, dt):
            return ctx.enter_context(nc.sbuf_tensor(name, shape, dt))

        def psum(name, shape, dt):
            return ctx.enter_context(nc.psum_tensor(name, shape, dt))

        def sem(name):
            return ctx.enter_context(nc.semaphore(name))

        wq16 = sb("wq16", [P, 2, CC, 3 * C], F16)
        wuT = sb("wuT", [P, CC, FF], F16)
        wdT = sb("wdT", [P, FC, C], F16)
        bias = sb("bias", [P, 3, C], F32)
        ident = sb("ident", [P, P], F16)
        octets = sb("octets", [P, P], F16)
        ident32 = sb("ident32", [P, P], F32)
        blocks = sb("blocks", [P, P], F32)
        half = sb("half", [P, 2 * TILES], F32)
        cst = sb("cst", [P, 24], F32)
        x_next = sb("x_next", [P, TILES, C], F32)
        xf = sb("xf", [P, 2, C], F32)
        xs = sb("xs", [P, 2, 2, C], F16)
        xT = sb("xT", [P, 2, CC, GT], F16)
        stats = sb("stats", [P, TILES, 6], F32)
        mv = sb("mv", [P, 4, TILES], F32)
        var2 = sb("var2", [P, 2 * TILES], F32)
        root = sb("root", [P, 2 * TILES], F32)
        ln = sb("ln", [P, 8, TILES], F32)
        hn = sb("hn", [P, 4, TILES], F32)
        inv_sd, rms, inv_rms, x_gain, q_gain, k_gain, v_gain = (ln[:, n, :] for n in range(7))
        mean, m_sum, m_diff, v_sum = (mv[:, n] for n in range(4))
        h_sum, h_root, h_gain = (hn[:, n, :] for n in range(3))
        kmax = sb("kmax", [P, HEADS], F32)
        ksum = sb("ksum", [P, HEADS], F32)
        kinv = sb("kinv", [P, HEADS], F32)

        region = sb("region", [P, 116 * 256], F32)
        pre = carve(region, {
            "wqkv": ((CC, 3 * C), F32), "wup": ((FC, C), F32), "wdn": ((CC, FF), F32),
            "tup": ((FC, C), F16)})
        pre["tdn"] = carve(region, {"tdn": ((CC, FF), F16)})["tdn"]
        work = carve(region, {
            "hT": ((2, FC, GT), F16), "hf": ((2, 2 * GT), F32), "hsq": ((2, GT), F32),
            "hpart": ((2, GT), F32), "hacc": ((GT,), F32), "xres": ((TILES, C), F32),
            "KT": ((2, P, HEADS), F16), "QT": ((2, P, HEADS), F16),
            "V16": ((TILES, 2, C), F16), "af": ((2, C), F32), "a_hi": ((OCT, P), F16),
            "a_lo": ((OCT, P), F16), "kr": ((HEADS, D), F32), "qr": ((HEADS, D), F32),
            "vr": ((C,), F32), "v1": ((C,), F32), "o1": ((C,), F32), "o2": ((C,), F32),
            "K16": ((HEADS, 4, D), F16), "Q16": ((HEADS, 4, D), F16)})
        hT, hf, hsq, hpart, hacc, xres = (work[n] for n in ("hT", "hf", "hsq", "hpart", "hacc", "xres"))
        KT, QT, V16, af, a_hi, a_lo = (work[n] for n in ("KT", "QT", "V16", "af", "a_hi", "a_lo"))
        kr, qr, vr, v1, o1, o2, K16, Q16 = (work[n] for n in ("kr", "qr", "vr", "v1", "o1", "o2", "K16", "Q16"))

        proj = [psum(f"proj{n}", [P, C], F32) for n in range(2)]
        ud = [psum(f"ud{n}", [P, GT], F32) for n in range(2)]
        tp = [psum(f"tp{n}", [P, 2 * GT], F16) for n in range(2)]
        sc = psum("sc", [P, 4, P], F32)
        ov = psum("ov", [P, OCT, D], F32)

        amax = cst[:, 0:2]
        asum = cst[:, 2:4]
        gmax = cst[:, 4:6]
        gsum = cst[:, 6:8]
        thr = cst[:, 8:10]
        nthr = cst[:, 10:12]
        bound = cst[:, 12:14]
        pow2 = cst[:, 14:16]
        ipow2 = cst[:, 16:18]
        w_gain, w_unit, qv_gain, q_mul, v_mul, o_unit = (cst[:, n:n + 1] for n in range(18, 24))
        qb_gain = ln[:, 7, 0:1]

        wqkv_in, bias_in, wup_in, wdn_in = sem("wqkv_in"), sem("bias_in"), sem("wup_in"), sem("wdn_in")
        consts_made = sem("consts_made")
        max_done, sum_done = sem("max_done"), sem("sum_done")
        consts_step, pre_thr, tern_step = sem("consts_step"), sem("pre_thr"), sem("tern_step")
        w_gain_ready = sem("w_gain_ready")
        abs_all = sem("abs_all")
        pre_step = sem("pre_step")
        gains_ready = sem("gains_ready")
        wq_hi_ready, wq_lo_ready = sem("wq_hi_ready"), sem("wq_lo_ready")
        tern_ready = sem("tern_ready")
        wt_turned = sem("wt_turned")
        wt_out_act, wt_out_dve = sem("wt_out_act"), sem("wt_out_dve")
        x_loaded = sem("x_loaded")
        stored = sem("stored")
        ln_step = sem("ln_step")
        ln_roots = sem("ln_roots")
        ln_in = sem("ln_in")
        xf_ready, xhi_ready, xlo_ready = sem("xf_ready"), sem("xhi_ready"), sem("xlo_ready")
        x_turned, xT_ready, res_ready = sem("x_turned"), sem("xT_ready"), sem("res_ready")
        proj_done, proj_out = sem("proj_done"), sem("proj_out")
        kmax_ready, kd_ready, ke_ready, ks_ready = sem("kmax_ready"), sem("kd_ready"), sem("ke_ready"), sem("ks_ready")
        kinv_ready, kn_ready, khi_ready, klo_ready = sem("kinv_ready"), sem("kn_ready"), sem("khi_ready"), sem("klo_ready")
        qhi_ready, qlo_ready = sem("qhi_ready"), sem("qlo_ready")
        k_parts, q_parts = sem("k_parts"), sem("q_parts")
        v1_ready, v2_ready, vhi_ready, vlo_ready = sem("v1_ready"), sem("v2_ready"), sem("vhi_ready"), sem("vlo_ready")
        qk_turned, qkT_ready = sem("qk_turned"), sem("qkT_ready")
        sc_done, af_ready, ahi_ready, alo_ready, av_done = (
            sem("sc_done"), sem("af_ready"), sem("ahi_ready"), sem("alo_ready"), sem("av_done"))
        o1_ready, o2_ready, xo_ready = sem("o1_ready"), sem("o2_ready"), sem("xo_ready")
        up_done, gelu_done = sem("up_done"), sem("gelu_done")
        hsq_ready, hhi_ready, hlo_ready, hpart_ready = (
            sem("hsq_ready"), sem("hhi_ready"), sem("hlo_ready"), sem("hpart_ready"))
        hacc_ready = sem("hacc_ready")
        ss_turned, ss_ready, ss_root = sem("ss_turned"), sem("ss_ready"), sem("ss_root")
        hg_step = sem("hg_step")
        down_done, final_ready = sem("down_done"), sem("final_ready")
        LN_STEPS = 11

        def wait_if_any(engine, semaphore, value):
            if not isinstance(value, int) or value > 0:
                engine.wait_ge(semaphore, value)

        block = ctx.enter_context(nc.Block())

        @block.sync
        def _(sp):
            sp.dma_start(x_next[:], x_groups[0]).then_inc(x_loaded, 16)
            sp.dma_start(pre["wqkv"], w_qkv.rearrange("(c p) n -> p c n", p=P)).then_inc(wqkv_in, 16)
            sp.dma_start(bias[:].rearrange("p a b -> p (a b)"),
                         b_qkv.rearrange("(a n) -> a n", a=1).partition_broadcast(P)).then_inc(bias_in, 16)
            sp.dma_start(pre["wup"], w_up.rearrange("(f p) c -> p f c", p=P)).then_inc(wup_in, 16)
            sp.dma_start(pre["wdn"], w_down.rearrange("(c p) f -> p c f", p=P)).then_inc(wdn_in, 16)

            def group(s, more):
                if more:
                    sp.wait_ge(res_ready, 4 * s + 4)
                    sp.wait_ge(xf_ready, 4 * s + 4)
                    sp.dma_start(x_next[:], x_groups[s + 1]).then_inc(x_loaded, 16)
                for i in range(TILES):
                    sp.wait_ge(final_ready, 4 * s + i + 1)
                    sp.dma_start(out_tiles[s, i], xres[:, i]).then_inc(stored, 16)

            group(0, True)
            with sp.Fori(1, GROUPS - 1) as s:
                group(s, True)
            group(GROUPS - 1, False)
            sp.wait_ge(stored, 64 * GROUPS)

        @block.tensor
        def _(pe):
            def turn_weights():
                pe.wait_ge(consts_made, 5)
                for n in range(16):
                    if n % 8 == 0:
                        pe.wait_ge(tern_ready, n // 8 + 1)
                    if n >= 2:
                        pe.wait_ge(wt_out_dve if n % 2 else wt_out_act, n // 2)
                    for m in range(8):
                        if n < 8:
                            src = pre["tup"][:, 8 * (n % 2) + m, (n // 2) * P:(n // 2 + 1) * P]
                        else:
                            f = 2 * (n - 8) + m // 4
                            src = pre["tdn"][:, m % 4, f * P:(f + 1) * P]
                        last = pe.transpose(tp[n % 2][:, m * P:(m + 1) * P], src, ident[:])
                    last.then_inc(wt_turned, 1)

            def turn_x(g, i, first=False):
                pe.wait_ge(xlo_ready, 4 * g + i + 1)
                if i >= 2:
                    pe.wait_ge(xT_ready, 4 * g + i - 1)
                elif first:
                    pe.wait_ge(wt_out_dve if i else wt_out_act, 8)
                else:
                    pe.wait_ge(qkT_ready, 16 * g - 1 + i)
                for part in range(2):
                    for c in range(CC):
                        last = pe.transpose(tp[i % 2][:, (part * CC + c) * P:(part * CC + c + 1) * P],
                                            xs[:, i % 2, part, c * P:(c + 1) * P], ident[:])
                last.then_inc(x_turned, 1)

            def project(s, i, m, col):
                n = 3 * i + m
                if m == 0:
                    pe.wait_ge(xT_ready, 4 * s + i + 1)
                wait_if_any(pe, proj_out, 12 * s + max(n - 1, 0))
                k = 0
                for c in range(CC):
                    for part, wpart in ((0, 0), (0, 1), (1, 0)):
                        last = pe.matmul(proj[n % 2][:], xT[:, part, c, i * P:(i + 1) * P],
                                         wq16[:, wpart, c, col * C:(col + 1) * C],
                                         start=(k == 0), stop=(k == 3 * CC - 1))
                        k += 1
                last.then_inc(proj_done, 1)

            def up(s, f):
                if f == 0:
                    pe.wait_ge(xT_ready, 4 * s + 4)
                if f < 2:
                    wait_if_any(pe, final_ready, 4 * s)
                else:
                    pe.wait_ge(gelu_done, 16 * s + f - 1)
                for c in range(CC):
                    for part in range(2):
                        last = pe.matmul(ud[f % 2][:], wuT[:, c, f * P:(f + 1) * P], xT[:, part, c, :],
                                         start=(c == 0 and part == 0), stop=(c == CC - 1 and part == 1))
                last.then_inc(up_done, 1)

            def turn_qk(s, i, j):
                n = 4 * i + j
                pe.wait_ge(k_parts if j < 2 else q_parts, 4 * s + i + 1)
                if n >= 2:
                    pe.wait_ge(qkT_ready, 16 * s + n - 1)
                for m in range(8):
                    h = 8 * (j % 2) + m
                    src = (K16 if j < 2 else Q16)[:, h].rearrange("p a d -> p (a d)")
                    last = pe.transpose(tp[n % 2][:, m * P:(m + 1) * P], src, octets[:])
                last.then_inc(qk_turned, 1)

            def scores(s, i, j):
                n = 4 * i + j
                pe.wait_ge(qkT_ready, 16 * s + 4 * i + 4)
                wait_if_any(pe, af_ready, 16 * s + n)
                for m in range(4):
                    octet = slice(8 * (4 * j + m), 8 * (4 * j + m + 1))
                    last = pe.matmul(sc[:, m], KT[:, i % 2, octet].rearrange("p t h -> p (t h)"),
                                     QT[:, i % 2, octet].rearrange("p t h -> p (t h)"), start=True, stop=True)
                last.then_inc(sc_done, 1)

            def weigh(s, i, j):
                pe.wait_ge(alo_ready, 16 * s + 4 * i + j + 1)
                if j == 0:
                    pe.wait_ge(vlo_ready, 4 * s + i + 1)
                    wait_if_any(pe, o1_ready, 4 * s + i)
                for n in range(4 * j, 4 * j + 4):
                    k = 0
                    for a in (a_hi, a_lo):
                        for part in range(2):
                            last = pe.matmul(ov[:, n], a[:, n], V16[:, i, part, n * D:(n + 1) * D],
                                             start=(k == 0), stop=(k == 3))
                            k += 1
                last.then_inc(av_done, 1)

            def down(s, i, g):
                if i == 0:
                    if g == 0:
                        pe.wait_ge(gelu_done, 16 * s + 15)
                    pe.wait_ge(hlo_ready, 8 * s + g + 1)
                elif g == 0:
                    if i == 1:
                        pe.wait_ge(ss_ready, s + 1)
                    else:
                        pe.wait_ge(final_ready, 4 * s + i - 1)
                for f in (2 * g, 2 * g + 1):
                    for part in range(2):
                        last = pe.matmul(ud[i % 2][:], hT[:, part, f, i * P:(i + 1) * P], wdT[:, f, :],
                                         start=(f == 0 and part == 0), stop=(f == FC - 1 and part == 1))
                if g == PAIRS - 1:
                    last.then_inc(down_done, 1)

            def turn_sums(s):
                pe.wait_ge(gelu_done, 16 * s + 16)
                pe.wait_ge(hacc_ready, 7 * s + 7)
                for i in range(TILES):
                    last = pe.transpose(ud[1][:, i * P:(i + 1) * P], hacc[:, i * P:(i + 1) * P], ident32[:])
                last.then_inc(ss_turned, 1)

            def group(s, more):
                for n in range(4):
                    def attend(turned=None, weighed=None, scored=None):
                        if weighed is not None and n >= 3:
                            weigh(s, n - 3, weighed)
                        if scored is not None and n >= 2:
                            scores(s, n - 2, scored)
                        if turned is not None and n >= 1:
                            turn_qk(s, n - 1, turned)
                    project(s, n, 0, 1)
                    attend(turned=0, weighed=0)
                    up(s, 4 * n)
                    attend(turned=1, weighed=1, scored=0)
                    project(s, n, 1, 0)
                    attend(turned=2, weighed=2, scored=1)
                    up(s, 4 * n + 1)
                    attend(turned=3, weighed=3)
                    project(s, n, 2, 2)
                    attend(scored=2)
                    up(s, 4 * n + 2)
                    attend(scored=3)
                    up(s, 4 * n + 3)
                fill = {
                    0: {0: [(turn_qk, 3, 0), (weigh, 1, 0)], 1: [(turn_qk, 3, 1), (weigh, 1, 1)],
                        2: [(scores, 2, 0), (turn_qk, 3, 2), (weigh, 1, 2)],
                        3: [(turn_qk, 3, 3), (weigh, 1, 3)], 4: [(scores, 2, 1)],
                        6: [(scores, 2, 2)], 7: [(scores, 2, 3)]},
                    1: {1: [(weigh, 2, 0), (scores, 3, 0)], 3: [(weigh, 2, 1), (scores, 3, 1)],
                        5: [(weigh, 2, 2), (scores, 3, 2)], 6: [(weigh, 2, 3)], 7: [(scores, 3, 3)]},
                    2: {3: [(weigh, 3, 0)], 4: [(weigh, 3, 1)], 5: [(weigh, 3, 2)], 6: [(weigh, 3, 3)]},
                    3: {}}
                turned = {(2, 1): 0, (2, 6): 1, (3, 2): 2, (3, 5): 3}
                for i in range(TILES):
                    for g in range(PAIRS):
                        down(s, i, g)
                        for piece, tile, j in fill[i].get(g, ()):
                            piece(s, tile, j)
                        if i == 0 and g == 5:
                            turn_sums(s)
                        if more and (i, g) in turned:
                            turn_x(s + 1, turned[i, g])

            turn_weights()
            for i in range(TILES):
                turn_x(0, i, first=True)
            pe.wait_ge(wq_lo_ready, 1)
            pe.wait_ge(wt_out_act, 8)
            pe.wait_ge(wt_out_dve, 8)
            group(0, True)
            with pe.Fori(1, GROUPS - 1) as s:
                group(s, True)
            group(GROUPS - 1, False)

        @block.vector
        def _(dve):
            def prepare():
                steps = [0]

                def then(ins):
                    steps[0] += 1
                    ins.then_inc(pre_step, 1)
                    dve.wait_ge(pre_step, steps[0])

                dve.wait_ge(wqkv_in, 16)
                dve.tensor_reduce(amax[:, 0:1], pre["wqkv"], AX.XY, ALU.max,
                                  apply_absolute_value=True).then_inc(max_done, 1)
                dve.wait_ge(bias_in, 16)
                dve.tensor_reduce(amax[:, 1:2], bias[:], AX.XY, ALU.max,
                                  apply_absolute_value=True).then_inc(max_done, 1)
                dve.wait_ge(abs_all, 1)
                then(dve.tensor_scalar(bound[:, 0:1], gmax[:, 0:1], TINY, None, ALU.max))
                then(dve.scalar_tensor_tensor(out=bound[:, 1:2], in0=bound[:, 0:1], scalar=float(C),
                                              in1=gmax[:, 1:2], op0=ALU.mult, op1=ALU.add))
                then(dve.tensor_scalar(pow2.bitcast(U32), bound.bitcast(U32), 0x7F800000, None, ALU.bitwise_and))
                then(dve.reciprocal(ipow2, pow2))
                dve.tensor_scalar(w_gain, ipow2[:, 0:1], TOP, None, ALU.mult)
                dve.tensor_scalar(w_unit, pow2[:, 0:1], 1.0 / (TOP * X_SCALE), None, ALU.mult)
                dve.tensor_scalar(qv_gain, ipow2[:, 1:2], TOP, None, ALU.mult)
                then(dve.tensor_scalar(o_unit, pow2[:, 1:2], 1.0 / TOP, None, ALU.mult))
                dve.tensor_tensor(v_mul, w_unit, qv_gain, ALU.mult)
                then(dve.tensor_scalar(qb_gain, qv_gain, SCALE, None, ALU.mult))
                dve.tensor_tensor(o_unit, o_unit, o_unit, ALU.mult)
                dve.tensor_scalar(bias[:, 2], bias[:, 2], qv_gain, None, ALU.mult)
                dve.tensor_scalar(bias[:, 0], bias[:, 0], qb_gain, None, ALU.mult)
                dve.tensor_tensor(q_mul, w_unit, qb_gain, ALU.mult).then_inc(w_gain_ready, 1)
                dve.wait_ge(w_gain_ready, 1)

            def prepare_rest():
                dve.wait_ge(wq_hi_ready, 1)
                dve.scalar_tensor_tensor(out=wq16[:, 1].rearrange("p c n -> p (c n)"),
                                         in0=pre["wqkv"].rearrange("p c n -> p (c n)"), scalar=w_gain,
                                         in1=wq16[:, 0].rearrange("p c n -> p (c n)"),
                                         op0=ALU.mult, op1=ALU.subtract).then_inc(wq_lo_ready, 1)
                dve.wait_ge(abs_all, 2)
                dve.tensor_scalar(thr, gsum, 0.5 / (FF * C), None, ALU.mult).then_inc(pre_thr, 1)
                dve.tensor_scalar(nthr, gsum, -0.5 / (FF * C), None, ALU.mult).then_inc(pre_thr, 1)
                dve.wait_ge(pre_thr, 2)
                for n, (w, t) in enumerate((("wup", "tup"), ("wdn", "tdn"))):
                    wf = pre[w].rearrange("p a b -> p (a b)")
                    tf = pre[t].rearrange("p a b -> p (a b)")
                    dve.tensor_scalar(tf, wf, nthr[:, n:n + 1], None, ALU.is_lt).then_inc(tern_step, 1)
                    dve.wait_ge(tern_step, n + 1)
                    dve.scalar_tensor_tensor(out=tf, in0=wf, scalar=thr[:, n:n + 1], in1=tf,
                                             op0=ALU.is_gt, op1=ALU.subtract).then_inc(tern_ready, 1)
                for n in range(1, 16, 2):
                    dve.wait_ge(wt_turned, n + 1)
                    dst = (wuT[:, n // 2, 1024 * (n % 2):1024 * (n % 2) + 1024] if n < 8 else
                           wdT[:, 2 * (n - 8):2 * (n - 8) + 2].rearrange("p a b -> p (a b)"))
                    dve.tensor_copy(dst, tp[n % 2][:]).then_inc(wt_out_dve, 1)

            def ln_stats(g, pair):
                dve.wait_ge(x_loaded, 16 * g + 16)
                for i in range(2 * pair, 2 * pair + 2):
                    dve.bn_stats(stats[:, i], x_next[:, i]).then_inc(ln_step, 1)

            def ln_var(g):
                dve.wait_ge(ln_step, LN_STEPS * g + 4)
                dve.tensor_tensor(m_sum, stats[:, :, 1], stats[:, :, 4], ALU.add)
                dve.tensor_tensor(m_diff, stats[:, :, 1], stats[:, :, 4], ALU.subtract)
                dve.tensor_tensor(v_sum, stats[:, :, 2], stats[:, :, 5], ALU.add).then_inc(ln_step, 1)
                dve.wait_ge(ln_step, LN_STEPS * g + 5)
                dve.tensor_scalar(mean, m_sum, 0.5, None, ALU.mult)
                dve.scalar_tensor_tensor(out=m_diff, in0=m_diff, scalar=0.25, in1=m_diff,
                                         op0=ALU.mult, op1=ALU.mult).then_inc(ln_step, 1)
                dve.wait_ge(ln_step, LN_STEPS * g + 6)
                dve.scalar_tensor_tensor(out=var2[:, TILES:], in0=v_sum, scalar=1.0 / C, in1=m_diff,
                                         op0=ALU.mult, op1=ALU.add).then_inc(ln_step, 1)
                dve.wait_ge(ln_step, LN_STEPS * g + 7)
                dve.tensor_scalar(var2[:, 0:TILES], var2[:, TILES:], LN_EPS, None, ALU.add).then_inc(ln_in, 1)

            def ln_gains(g):
                dve.wait_ge(ln_roots, g + 1)
                dve.reciprocal(inv_sd, root[:, 0:TILES]).then_inc(ln_step, 1)
                dve.wait_ge(ln_step, LN_STEPS * g + 8)
                dve.tensor_tensor(rms, root[:, TILES:], inv_sd, ALU.mult).then_inc(ln_step, 1)
                dve.wait_ge(ln_step, LN_STEPS * g + 9)
                dve.tensor_scalar(rms, rms, RMS_EPS, None, ALU.add).then_inc(ln_step, 1)
                dve.wait_ge(ln_step, LN_STEPS * g + 10)
                dve.reciprocal(inv_rms, rms).then_inc(ln_step, 1)
                dve.tensor_scalar(q_gain, rms, q_mul, None, ALU.mult)
                dve.tensor_scalar(k_gain, rms, w_unit, None, ALU.mult)
                dve.tensor_scalar(v_gain, rms, v_mul, None, ALU.mult).then_inc(gains_ready, 1)
                dve.wait_ge(ln_step, LN_STEPS * g + 11)
                dve.scalar_tensor_tensor(out=x_gain, in0=inv_sd, scalar=X_SCALE, in1=inv_rms,
                                         op0=ALU.mult, op1=ALU.mult).then_inc(gains_ready, 1)

            def normalise(g, i):
                if i == 0:
                    dve.wait_ge(gains_ready, 2 * g + 2)
                wait_if_any(dve, xlo_ready, 4 * g + max(i - 1, 0))
                dve.tensor_scalar(xf[:, i % 2], x_next[:, i], mean[:, i:i + 1], x_gain[:, i:i + 1],
                                  ALU.subtract, ALU.mult).then_inc(xf_ready, 1)

            def proj_to(dst, s, i, m, col, gain):
                n = 3 * i + m
                dve.wait_ge(proj_done, 12 * s + n + 1)
                dve.scalar_tensor_tensor(out=dst, in0=proj[n % 2][:], scalar=gain[:, i:i + 1],
                                         in1=bias[:, col], op0=ALU.mult, op1=ALU.add).then_inc(proj_out, 1)

            def k_first(s, i):
                if i == 0:
                    dve.wait_ge(gains_ready, 2 * s + 2)
                wait_if_any(dve, klo_ready, 4 * s + i)
                proj_to(kr.rearrange("p h d -> p (h d)"), s, i, 0, 1, k_gain)
                dve.wait_ge(proj_out, 12 * s + 3 * i + 1)
                dve.tensor_reduce(kmax[:], kr, AX.X, ALU.max).then_inc(kmax_ready, 1)
                dve.wait_ge(kmax_ready, 4 * s + i + 1)
                dve.tensor_tensor(kr, kr, kmax[:].unsqueeze(2).broadcast_to([P, HEADS, D]),
                                  ALU.subtract).then_inc(kd_ready, 1)

            def k_sum(s, i):
                dve.wait_ge(ke_ready, 4 * s + i + 1)
                wait_if_any(dve, kn_ready, 4 * s + i)
                dve.tensor_reduce(ksum[:], kr, AX.X, ALU.add).then_inc(ks_ready, 1)
                dve.wait_ge(ks_ready, 8 * s + 2 * i + 1)
                dve.tensor_scalar(ksum[:], ksum[:], 1.0 / K_SCALE, None, ALU.mult).then_inc(ks_ready, 1)
                dve.wait_ge(ks_ready, 8 * s + 2 * i + 2)
                dve.reciprocal(kinv[:], ksum[:]).then_inc(kinv_ready, 1)

            def q_first(s, i):
                wait_if_any(dve, qlo_ready, 4 * s + i)
                proj_to(qr.rearrange("p h d -> p (h d)"), s, i, 1, 0, q_gain)

            def fill_k(s, i):
                dve.wait_ge(klo_ready, 4 * s + i + 1)
                dve.tensor_copy(K16[:, :, 3], K16[:, :, 2]).then_inc(k_parts, 1)

            def fill_q(s, i):
                dve.wait_ge(qlo_ready, 4 * s + i + 1)
                dve.tensor_copy(Q16[:, :, 3], Q16[:, :, 1]).then_inc(q_parts, 1)

            def v_first(s, i):
                wait_if_any(dve, vlo_ready, 4 * s + i)
                proj_to(vr, s, i, 2, 2, v_gain)
                dve.wait_ge(proj_out, 12 * s + 3 * i + 3)
                dve.transpose(v1, vr).then_inc(v1_ready, 1)
                dve.wait_ge(v1_ready, 4 * s + i + 1)
                dve.transpose(vr.rearrange("p (n a b) -> p n a b", n=OCT, a=2),
                              v1.rearrange("p (g n two) -> p n two g", g=HEADS, two=2)).then_inc(v2_ready, 1)

            def mask(s, i, j):
                n = 4 * i + j
                dve.wait_ge(sc_done, 16 * s + n + 1)
                wait_if_any(dve, alo_ready, 16 * s + max(n - 1, 0))
                dve.tensor_tensor(af[:, j % 2].rearrange("p (m n) -> p m n", m=4), sc[:],
                                  blocks[:].unsqueeze(1).broadcast_to([P, 4, P]),
                                  ALU.mult).then_inc(af_ready, 1)

            def h_parts(s, p):
                hp = hf[:, p % 2]
                dst = [hT[:, part, 2 * p:2 * p + 2].rearrange("p a b -> p (a b)") for part in range(2)]
                if p == 0:
                    wait_if_any(dve, down_done, 4 * s)
                dve.wait_ge(gelu_done, 16 * s + 2 * p + 2)
                dve.tensor_scalar(dst[0], hp, H_SCALE, None, ALU.mult).then_inc(hhi_ready, 1)
                dve.wait_ge(hhi_ready, 8 * s + p + 1)
                dve.scalar_tensor_tensor(out=dst[1], in0=hp, scalar=H_SCALE, in1=dst[0],
                                         op0=ALU.mult, op1=ALU.subtract).then_inc(hlo_ready, 1)

            def h_squares(s, p):
                dve.wait_ge(hsq_ready, 8 * s + p + 1)
                wait_if_any(dve, hacc_ready, 7 * s + (0 if p < 2 else max(p - 2, 1)))
                dve.tensor_tensor(hpart[:, p % 2], hsq[:, 0], hsq[:, 1], ALU.add).then_inc(hpart_ready, 1)

            def out_turn(s, i):
                dve.wait_ge(av_done, 16 * s + 4 * i + 4)
                dve.transpose(o1, ov[:].rearrange("p n d -> p (n d)")).then_inc(o1_ready, 1)
                dve.wait_ge(o1_ready, 4 * s + i + 1)
                dve.transpose(o2.rearrange("p (h d) -> p h d", h=HEADS),
                              o1.rearrange("p (t h) -> p h t", h=HEADS)).then_inc(o2_ready, 1)

            def add_x(s, i):
                dve.wait_ge(res_ready, 4 * s + i + 1)
                dve.wait_ge(o2_ready, 4 * s + i + 1)
                dve.scalar_tensor_tensor(out=xres[:, i], in0=o2, scalar=o_unit, in1=xres[:, i],
                                         op0=ALU.mult, op1=ALU.add).then_inc(xo_ready, 1)

            def sum_squares(s):
                dve.wait_ge(ss_turned, s + 1)
                dve.tensor_reduce(h_sum, ud[1][:].rearrange("p (i f) -> p i f", i=TILES), AX.X,
                                  ALU.add).then_inc(ss_ready, 1)

            def h_gains(s):
                dve.wait_ge(ss_root, s + 1)
                dve.tensor_scalar(h_root, h_root, float(FF) ** -0.5, RMS_EPS, ALU.mult, ALU.add).then_inc(hg_step, 1)
                dve.wait_ge(hg_step, 3 * s + 1)
                dve.reciprocal(h_gain, h_root).then_inc(hg_step, 1)
                dve.wait_ge(hg_step, 3 * s + 2)
                dve.tensor_scalar(h_gain, h_gain, 1.0 / H_SCALE, None, ALU.mult).then_inc(hg_step, 1)
                dve.wait_ge(hg_step, 3 * s + 3)

            def final(s, i):
                dve.wait_ge(down_done, 4 * s + i + 1)
                dve.wait_ge(xo_ready, 4 * s + i + 1)
                dve.scalar_tensor_tensor(out=xres[:, i], in0=ud[i % 2][:], scalar=h_gain[:, i:i + 1],
                                         in1=xres[:, i], op0=ALU.mult, op1=ALU.add).then_inc(final_ready, 1)

            def group(s, more):
                for n in range(4):
                    def mask_quarter(j):
                        if n >= 2:
                            mask(s, n - 2, j)
                    k_first(s, n)
                    mask_quarter(0)
                    k_sum(s, n)
                    mask_quarter(1)
                    q_first(s, n)
                    h_parts(s, 2 * n)
                    mask_quarter(2)
                    h_squares(s, 2 * n)
                    fill_k(s, n)
                    v_first(s, n)
                    mask_quarter(3)
                    fill_q(s, n)
                    if n == 3:
                        out_turn(s, 0)
                    h_parts(s, 2 * n + 1)
                    h_squares(s, 2 * n + 1)
                mask(s, 2, 0)
                add_x(s, 0)
                out_turn(s, 1)
                mask(s, 2, 1)
                if more:
                    ln_stats(s + 1, 0)
                sum_squares(s)
                mask(s, 2, 2)
                if more:
                    ln_stats(s + 1, 1)
                mask(s, 2, 3)
                if more:
                    ln_var(s + 1)
                mask(s, 3, 0)
                h_gains(s)
                final(s, 0)
                mask(s, 3, 1)
                add_x(s, 1)
                if more:
                    ln_gains(s + 1)
                    normalise(s + 1, 0)
                    normalise(s + 1, 1)
                mask(s, 3, 2)
                mask(s, 3, 3)
                final(s, 1)
                out_turn(s, 2)
                add_x(s, 2)
                if more:
                    normalise(s + 1, 2)
                    normalise(s + 1, 3)
                final(s, 2)
                out_turn(s, 3)
                add_x(s, 3)
                final(s, 3)

            prepare()
            ln_stats(0, 0)
            ln_stats(0, 1)
            ln_var(0)
            ln_gains(0)
            prepare_rest()
            for i in range(TILES):
                normalise(0, i)
            dve.wait_ge(wt_turned, 16)
            group(0, True)
            with dve.Fori(1, GROUPS - 1) as s:
                group(s, True)
            group(GROUPS - 1, False)

        @block.scalar
        def _(act):
            def prepare():
                for n, (w, s_in) in enumerate((("wup", wup_in), ("wdn", wdn_in))):
                    act.wait_ge(s_in, 16)
                    if n:
                        act.wait_ge(sum_done, 1)
                    act.activation(pre["tup"].rearrange("p a b -> p (a b)"), pre[w].rearrange("p a b -> p (a b)"),
                                   ACT.Abs, accum_out=asum[:, n:n + 1]).then_inc(sum_done, 1)
                    if n == 0:
                        act.wait_ge(w_gain_ready, 1)
                        act.activation(wq16[:, 0].rearrange("p c n -> p (c n)"),
                                       pre["wqkv"].rearrange("p c n -> p (c n)"), ACT.Copy,
                                       scale=w_gain).then_inc(wq_hi_ready, 1)

            def prepare_rest():
                for n in range(0, 16, 2):
                    act.wait_ge(wt_turned, n + 1)
                    dst = (wuT[:, n // 2, 0:1024] if n < 8 else
                           wdT[:, 2 * (n - 8):2 * (n - 8) + 2].rearrange("p a b -> p (a b)"))
                    act.copy(dst, tp[0][:]).then_inc(wt_out_act, 1)

            def x_hi(g, i):
                act.wait_ge(xf_ready, 4 * g + i + 1)
                wait_if_any(act, x_turned, 4 * g + max(i - 1, 0))
                act.copy(xs[:, i % 2, 0], xf[:, i % 2]).then_inc(xhi_ready, 1)

            def x_out(g, i):
                if i == 0:
                    wait_if_any(act, proj_done, 12 * g)
                    wait_if_any(act, up_done, 16 * g)
                act.wait_ge(x_turned, 4 * g + i + 1)
                act.copy(xT[:, :, :, i * P:(i + 1) * P],
                         tp[i % 2][:].rearrange("p (a c t) -> p a c t", a=2, c=CC)).then_inc(xT_ready, 1)

            def residual(s, i):
                if i == 0:
                    act.wait_ge(x_loaded, 16 * s + 16)
                    wait_if_any(act, stored, 64 * s)
                act.copy(xres[:, i], x_next[:, i]).then_inc(res_ready, 1)

            def qk_out(s, i, j):
                n = 4 * i + j
                if j == 0:
                    wait_if_any(act, sc_done, 16 * s + 4 * max(i - 1, 0))
                act.wait_ge(qk_turned, 16 * s + n + 1)
                dst = (KT if j < 2 else QT)[:, i % 2, :, 8 * (j % 2):8 * (j % 2) + 8]
                act.copy(dst, tp[n % 2][:].rearrange("p (h t) -> p t h", h=8)).then_inc(qkT_ready, 1)

            def gelu(s, f):
                p = f // 2
                wait_if_any(act, hlo_ready, 8 * s + max(p - 1, 0))
                act.wait_ge(up_done, 16 * s + f + 1)
                act.activation(hf[:, p % 2, (f % 2) * GT:(f % 2 + 1) * GT], ud[f % 2][:], ACT.Gelu,
                               scale=1.0 / X_SCALE).then_inc(gelu_done, 1)

            def square(s, p):
                act.wait_ge(gelu_done, 16 * s + 2 * p + 2)
                wait_if_any(act, hpart_ready, 8 * s + p)
                act.activation(hsq.rearrange("p a b -> p (a b)"), hf[:, p % 2], ACT.Square).then_inc(hsq_ready, 1)

            def q_hi(s, i):
                act.wait_ge(proj_out, 12 * s + 3 * i + 2)
                wait_if_any(act, qk_turned, 16 * s + 4 * i)
                act.copy(Q16[:, :, 0::2], qr.unsqueeze(2).broadcast_to([P, HEADS, 2, D])).then_inc(qhi_ready, 1)

            def k_exp(s, i):
                act.wait_ge(kd_ready, 4 * s + i + 1)
                act.activation(kr, kr, ACT.Exp).then_inc(ke_ready, 1)

            def k_hi(s, i):
                act.wait_ge(kn_ready, 4 * s + i + 1)
                wait_if_any(act, qk_turned, 16 * s + max(4 * i - 2, 0))
                act.copy(K16[:, :, 0:2], kr.unsqueeze(2).broadcast_to([P, HEADS, 2, D])).then_inc(khi_ready, 1)

            def v_hi(s, i):
                act.wait_ge(v2_ready, 4 * s + i + 1)
                wait_if_any(act, av_done, 16 * s)
                act.copy(V16[:, i, 0], vr).then_inc(vhi_ready, 1)

            def att_hi(s, i, j):
                n = 4 * i + j
                act.wait_ge(af_ready, 16 * s + n + 1)
                wait_if_any(act, av_done, 16 * s + max(n - 3, 0))
                act.copy(a_hi[:, 4 * j:4 * j + 4].rearrange("p a b -> p (a b)"), af[:, j % 2]).then_inc(ahi_ready, 1)

            def group(s, more):
                for n in range(4):
                    def turned(j):
                        if n >= 1:
                            qk_out(s, n - 1, j)

                    def weights(j):
                        if n >= 2:
                            att_hi(s, n - 2, j)
                    turned(0)
                    k_exp(s, n)
                    gelu(s, 4 * n)
                    turned(1)
                    weights(0)
                    turned(2)
                    weights(1)
                    k_hi(s, n)
                    gelu(s, 4 * n + 1)
                    square(s, 2 * n)
                    turned(3)
                    q_hi(s, n)
                    if n < 2:
                        residual(s, 2 * n)
                        residual(s, 2 * n + 1)
                    weights(2)
                    gelu(s, 4 * n + 2)
                    v_hi(s, n)
                    weights(3)
                    gelu(s, 4 * n + 3)
                    square(s, 2 * n + 1)
                for j in range(4):
                    qk_out(s, 3, j)
                    if j == 2:
                        att_hi(s, 2, 0)
                att_hi(s, 2, 1)
                att_hi(s, 2, 2)
                att_hi(s, 2, 3)
                att_hi(s, 3, 0)
                att_hi(s, 3, 1)
                if more:
                    x_hi(s + 1, 0)
                    x_hi(s + 1, 1)
                att_hi(s, 3, 2)
                att_hi(s, 3, 3)
                if more:
                    x_out(s + 1, 0)
                    x_hi(s + 1, 2)
                    x_out(s + 1, 1)
                    x_hi(s + 1, 3)
                    x_out(s + 1, 2)
                    x_out(s + 1, 3)

            prepare()
            prepare_rest()
            x_hi(0, 0)
            x_hi(0, 1)
            x_out(0, 0)
            x_hi(0, 2)
            x_out(0, 1)
            x_hi(0, 3)
            x_out(0, 2)
            x_out(0, 3)
            act.wait_ge(wt_turned, 16)
            act.wait_ge(wq_lo_ready, 1)
            group(0, True)
            with act.Fori(1, GROUPS - 1) as s:
                group(s, True)
            group(GROUPS - 1, False)

        @block.gpsimd
        def _(pool):
            def prepare():
                pool.memset(ident32[:], 1.0).then_inc(consts_step, 1)
                pool.memset(ident[:], 1.0).then_inc(consts_step, 1)
                pool.memset(octets[:], 1.0).then_inc(consts_step, 1)
                pool.memset(blocks[:], 1.0 / K_SCALE).then_inc(consts_step, 1)
                pool.memset(half[:], 0.5).then_inc(consts_made, 1)
                pool.wait_ge(consts_step, 4)
                pool.affine_select(out=ident32[:], in_=ident32[:], compare_op=ALU.is_equal, fill=0.0, base=0,
                                   pattern=[[-1, P]], channel_multiplier=1).then_inc(consts_made, 1)
                pool.affine_select(out=ident[:], in_=ident[:], compare_op=ALU.is_equal, fill=0.0, base=0,
                                   pattern=[[-1, P]], channel_multiplier=1).then_inc(consts_made, 1)
                o4 = octets[:].rearrange("p (n q two) -> p n q two", q=4, two=2)
                pool.affine_select(out=o4, in_=o4, compare_op=ALU.is_equal, fill=0.0, base=0,
                                   pattern=[[-2, OCT], [-32, 4], [-1, 2]],
                                   channel_multiplier=1).then_inc(consts_made, 1)
                b3 = blocks[:].rearrange("p (a b) -> p a b", b=HEADS)
                pool.affine_select(out=b3, in_=b3, compare_op=ALU.is_ge, fill=0.0, base=0,
                                   pattern=[[-HEADS, P // HEADS], [0, HEADS]],
                                   channel_multiplier=1).then_inc(consts_step, 1)
                pool.wait_ge(consts_step, 5)
                pool.affine_select(out=b3, in_=b3, compare_op=ALU.is_ge, fill=0.0, base=HEADS - 1,
                                   pattern=[[HEADS, P // HEADS], [0, HEADS]],
                                   channel_multiplier=-1).then_inc(consts_made, 1)
                pool.wait_ge(max_done, 2)
                pool.partition_all_reduce(gmax, amax, P, bass.bass_isa.ReduceOp.max).then_inc(abs_all, 1)
                ln_pow(0)
                pool.wait_ge(sum_done, 2)
                pool.partition_all_reduce(gsum, asum, P, bass.bass_isa.ReduceOp.add).then_inc(abs_all, 1)

            def ln_pow(g):
                pool.wait_ge(ln_in, g + 1)
                pool.tensor_tensor(root[:], var2[:], half[:], ALU.pow).then_inc(ln_roots, 1)

            def h_pow(s):
                pool.wait_ge(ss_ready, s + 1)
                pool.tensor_tensor(h_root, h_sum, half[:, 0:TILES], ALU.pow).then_inc(ss_root, 1)

            def x_lo(g, i):
                pool.wait_ge(xhi_ready, 4 * g + i + 1)
                pool.tensor_tensor(xs[:, i % 2, 1], xf[:, i % 2], xs[:, i % 2, 0],
                                   ALU.subtract).then_inc(xlo_ready, 1)

            def q_lo(s, i):
                pool.wait_ge(qhi_ready, 4 * s + i + 1)
                pool.tensor_tensor(Q16[:, :, 1], qr, Q16[:, :, 0], ALU.subtract).then_inc(qlo_ready, 1)

            def k_norm(s, i):
                pool.wait_ge(kinv_ready, 4 * s + i + 1)
                pool.tensor_tensor(kr, kr, kinv[:].unsqueeze(2).broadcast_to([P, HEADS, D]),
                                   ALU.mult).then_inc(kn_ready, 1)

            def k_lo(s, i):
                pool.wait_ge(khi_ready, 4 * s + i + 1)
                pool.tensor_tensor(K16[:, :, 2], kr, K16[:, :, 0], ALU.subtract).then_inc(klo_ready, 1)

            def v_lo(s, i):
                pool.wait_ge(vhi_ready, 4 * s + i + 1)
                pool.tensor_tensor(V16[:, i, 1], vr, V16[:, i, 0], ALU.subtract).then_inc(vlo_ready, 1)

            def att_lo(s, i, j):
                pool.wait_ge(ahi_ready, 16 * s + 4 * i + j + 1)
                pool.tensor_tensor(a_lo[:, 4 * j:4 * j + 4].rearrange("p a b -> p (a b)"), af[:, j % 2],
                                   a_hi[:, 4 * j:4 * j + 4].rearrange("p a b -> p (a b)"),
                                   ALU.subtract).then_inc(alo_ready, 1)

            def h_add(s, p):
                if p == 1:
                    wait_if_any(pool, ss_turned, s)
                else:
                    pool.wait_ge(hacc_ready, 7 * s + p - 1)
                pool.wait_ge(hpart_ready, 8 * s + p + 1)
                pool.tensor_tensor(hacc, hpart[:, 0] if p == 1 else hacc, hpart[:, p % 2],
                                   ALU.add).then_inc(hacc_ready, 1)

            def group(s, more):
                for n in range(4):
                    def weights(j):
                        if n >= 2:
                            att_lo(s, n - 2, j)
                    if n:
                        h_add(s, 2 * n - 1)
                    weights(0)
                    k_norm(s, n)
                    weights(1)
                    k_lo(s, n)
                    if n:
                        h_add(s, 2 * n)
                    q_lo(s, n)
                    weights(2)
                    v_lo(s, n)
                    weights(3)
                h_add(s, 7)
                for j in range(3):
                    att_lo(s, 2, j)
                h_pow(s)
                att_lo(s, 2, 3)
                if more:
                    ln_pow(s + 1)
                att_lo(s, 3, 0)
                att_lo(s, 3, 1)
                if more:
                    x_lo(s + 1, 0)
                    x_lo(s + 1, 1)
                att_lo(s, 3, 2)
                att_lo(s, 3, 3)
                if more:
                    x_lo(s + 1, 2)
                    x_lo(s + 1, 3)

            prepare()
            for i in range(TILES):
                x_lo(0, i)
            pool.wait_ge(wt_turned, 16)
            pool.wait_ge(wq_lo_ready, 1)
            group(0, True)
            with pool.Fori(1, GROUPS - 1) as s:
                group(s, True)
            group(GROUPS - 1, False)


_INS = ['L0_attn_x', 'L0_attn_W_qkv', 'L0_attn_b_qkv', 'L0_ffn_w_up', 'L0_ffn_w_down']
_OUTS = [((8, 1024, 512), 'float32')]


def kernel(**inputs):
    import numpy as _np
    import concourse.bacc as _bacc
    from concourse import mybir as _mybir
    from concourse.bass_utils import run_bass_kernel_spmd as _run

    nc = _bacc.Bacc("TRN2", target_bir_lowering=False, num_devices=1)
    arrays, args = {}, []
    for name in _INS:
        a = _np.ascontiguousarray(inputs[name])
        arrays[f"in_{name}_dram"] = a
        args.append(nc.dram_tensor(f"in_{name}_dram", a.shape, _mybir.dt.from_np(a.dtype), kind="ExternalInput").ap())
    for i, (shape, dtype) in enumerate(_OUTS):
        dt = _mybir.dt.from_np(_np.dtype(dtype))
        args.append(nc.dram_tensor(f"out_{i}_dram", shape, dt, kind="ExternalOutput").ap())
    layer_kernel(nc, *args)
    r = _run(nc, [arrays], core_ids=[0])
    return r.results[0]["out_0_dram"]
```

```python
from contextlib import ExitStack

import numpy as np

import concourse.bass as bass
from concourse import mybir

ALU = mybir.AluOpType
ACT = mybir.ActivationFunctionType
AX = mybir.AxisListType
F32 = mybir.dt.float32
F16 = mybir.dt.float16
U32 = mybir.dt.uint32

P = 128
HEADS = 16
X_SCALE = 2.0 ** 10
H_SCALE = 2.0 ** 6
K_SCALE = 2.0 ** 14
TOP = 2.0 ** 14
LN_EPS = 1e-5
RMS_EPS = 1e-8
TINY = 1e-30


def carve(region, sizes):
    out, at = {}, 0
    for name, (shape, dt) in sizes.items():
        words = int(np.prod(shape)) * (2 if dt == F16 else 4) // 4
        v = region[:, at:at + words]
        if dt != F32:
            v = v.bitcast(dt)
        if len(shape) == 2:
            v = v.rearrange("p (a b) -> p a b", a=shape[0])
        if len(shape) == 3:
            v = v.rearrange("p (a b c) -> p a b c", a=shape[0], b=shape[1])
        out[name] = v
        at += words
    assert at <= region.shape[1], (at, region.shape)
    return out


def layer_kernel(nc, x, w_qkv, b_qkv, w_up, w_down, out):
    batch, seq, C = x.shape
    TOKENS = batch * seq
    FF = w_up.shape[0]
    D = C // HEADS
    SCALE = float(D) ** -0.5
    TILES = 4
    GT = TILES * P
    GROUPS = TOKENS // GT
    CC = C // P
    FC = FF // P
    PAIRS = FC // 2
    OCT = P // 8
    assert C == 512 and D == 32 and FC == 16 and CC == 4

    x_groups = x.rearrange("a b c -> (a b) c").rearrange("(s i p) c -> s p i c", i=TILES, p=P)
    out_tiles = out.rearrange("a b c -> (a b) c").rearrange("(s i p) c -> s i p c", i=TILES, p=P)

    with ExitStack() as ctx:
        def sb(name, shape, dt):
            return ctx.enter_context(nc.sbuf_tensor(name, shape, dt))

        def psum(name, shape, dt):
            return ctx.enter_context(nc.psum_tensor(name, shape, dt))

        def sem(name):
            return ctx.enter_context(nc.semaphore(name))

        wq16 = sb("wq16", [P, 2, CC, 3 * C], F16)
        wuT = sb("wuT", [P, CC, FF], F16)
        wdT = sb("wdT", [P, FC, C], F16)
        bias = sb("bias", [P, 3, C], F32)
        ident = sb("ident", [P, P], F16)
        minus_ident = sb("minus_ident", [P, P], F16)
        octets = sb("octets", [P, P], F16)
        ident32 = sb("ident32", [P, P], F32)
        blocks = sb("blocks", [P, P], F32)
        half = sb("half", [P, 2 * TILES], F32)
        cst = sb("cst", [P, 24], F32)
        bias_rows = sb("bias_rows", [P, 3 * C // P], F32)
        parts = sb("parts", [P, 16], F32)
        g_parts = sb("g_parts", [P, 16], F32)
        x_next = sb("x_next", [P, TILES, C], F32)
        xf = sb("xf", [P, 2, C], F32)
        xs = sb("xs", [P, 2, 2, C], F16)
        xT = sb("xT", [P, 2, CC, GT], F16)
        stats = sb("stats", [P, TILES, 6], F32)
        mv = sb("mv", [P, 4, TILES], F32)
        var2 = sb("var2", [P, 2 * TILES], F32)
        root = sb("root", [P, 2 * TILES], F32)
        ln = sb("ln", [P, 8, TILES], F32)
        hn = sb("hn", [P, 4, TILES], F32)
        inv_sd, rms, inv_rms, x_gain, q_gain, k_gain, v_gain = (ln[:, n, :] for n in range(7))
        mean, m_sum, m_diff, v_sum = (mv[:, n] for n in range(4))
        h_sum, h_root, h_gain = (hn[:, n, :] for n in range(3))
        kmax = sb("kmax", [P, HEADS], F32)
        ksum = sb("ksum", [P, HEADS], F32)
        kinv = sb("kinv", [P, HEADS], F32)

        region = sb("region", [P, 116 * 256], F32)
        pre = carve(region, {
            "wqkv": ((CC, 3 * C), F32), "wup": ((FC, C), F32), "wdn": ((CC, FF), F32),
            "up_pos": ((FC, C), F16), "unread": ((3, FF), F16)})
        wup_at = CC * 3 * C
        pre.update(carve(region[:, wup_at:wup_at + FC * C], {"dn_pos": ((CC, FF), F16), "dn_neg": ((CC, FF), F16)}))
        pre["up_neg"] = wdT
        work = carve(region, {
            "hT": ((2, FC, GT), F16), "hf": ((2, 2 * GT), F32), "hsq": ((2, GT), F32),
            "hpart": ((2, GT), F32), "hacc": ((GT,), F32), "xres": ((TILES, C), F32),
            "KT": ((2, P, HEADS), F16), "QT": ((2, P, HEADS), F16),
            "V16": ((TILES, 2, C), F16), "af": ((2, C), F32), "a_hi": ((OCT, P), F16),
            "a_lo": ((OCT, P), F16), "kr": ((HEADS, D), F32), "qr": ((HEADS, D), F32),
            "vr": ((C,), F32), "v1": ((C,), F32), "o1": ((C,), F32), "o2": ((C,), F32),
            "K16": ((HEADS, 4, D), F16), "Q16": ((HEADS, 4, D), F16)})
        hT, hf, hsq, hpart, hacc, xres = (work[n] for n in ("hT", "hf", "hsq", "hpart", "hacc", "xres"))
        KT, QT, V16, af, a_hi, a_lo = (work[n] for n in ("KT", "QT", "V16", "af", "a_hi", "a_lo"))
        kr, qr, vr, v1, o1, o2, K16, Q16 = (work[n] for n in ("kr", "qr", "vr", "v1", "o1", "o2", "K16", "Q16"))

        proj = [psum(f"proj{n}", [P, C], F32) for n in range(2)]
        ud = [psum(f"ud{n}", [P, GT], F32) for n in range(2)]
        tp = [psum(f"tp{n}", [P, 2 * GT], F16) for n in range(2)]
        sc = psum("sc", [P, 4, P], F32)
        ov = psum("ov", [P, OCT, D], F32)

        w_banks = [ud[0][:], ud[1][:], sc[:].rearrange("p a b -> p (a b)"), ov[:].rearrange("p a b -> p (a b)")]

        w_max, b_max, up_sums, dn_sums = parts[:, 0:CC], parts[:, CC:CC + 1], parts[:, 5:9], parts[:, 9:13]
        g_max, g_bmax, g_up, g_dn = g_parts[:, 0:CC], g_parts[:, CC:CC + 1], g_parts[:, 5:9], g_parts[:, 9:13]
        gmax = cst[:, 0:1]
        gsum = cst[:, 2:4]
        thr = cst[:, 8:10]
        nthr = cst[:, 10:12]
        bound = cst[:, 12:14]
        pow2 = cst[:, 14:16]
        ipow2 = cst[:, 16:18]
        w_gain, w_unit, qv_gain, q_mul, v_mul, o_unit = (cst[:, n:n + 1] for n in range(18, 24))
        qb_gain = ln[:, 7, 0:1]

        bias_in, bias_rows_in = sem("bias_in"), sem("bias_rows_in")
        wqkv_in = [sem(f"wqkv_in{c}") for c in range(CC)]
        wup_in = [sem(f"wup_in{c}") for c in range(4)]
        wdn_in = [sem(f"wdn_in{c}") for c in range(CC)]
        consts_made = sem("consts_made")
        max_done = sem("max_done")
        up_sum_done, dn_sum_done = sem("up_sum_done"), sem("dn_sum_done")
        consts_step, pre_thr = sem("consts_step"), sem("pre_thr")
        w_gain_ready = sem("w_gain_ready")
        abs_all = sem("abs_all")
        pre_step = sem("pre_step")
        x_gain_ready, gains_ready = sem("x_gain_ready"), sem("gains_ready")
        wq_hi_ready, wq_lo_ready = sem("wq_hi_ready"), sem("wq_lo_ready")
        masks_ready = sem("masks_ready")
        wt_turned = sem("wt_turned")
        wt_out = sem("wt_out")
        x_loaded = sem("x_loaded")
        stored = sem("stored")
        ln_step = sem("ln_step")
        ln_roots = sem("ln_roots")
        ln_in = sem("ln_in")
        xf_ready, xhi_ready, xlo_ready = sem("xf_ready"), sem("xhi_ready"), sem("xlo_ready")
        x_turned, xT_ready, res_ready = sem("x_turned"), sem("xT_ready"), sem("res_ready")
        proj_done, proj_out = sem("proj_done"), sem("proj_out")
        kmax_ready, kd_ready, ke_ready, ks_ready = sem("kmax_ready"), sem("kd_ready"), sem("ke_ready"), sem("ks_ready")
        kinv_ready, kn_ready, khi_ready, klo_ready = sem("kinv_ready"), sem("kn_ready"), sem("khi_ready"), sem("klo_ready")
        qhi_ready, qlo_ready = sem("qhi_ready"), sem("qlo_ready")
        k_parts, q_parts = sem("k_parts"), sem("q_parts")
        v1_ready, v2_ready, vhi_ready, vlo_ready = sem("v1_ready"), sem("v2_ready"), sem("vhi_ready"), sem("vlo_ready")
        qk_turned, qkT_ready = sem("qk_turned"), sem("qkT_ready")
        sc_done, af_ready, ahi_ready, alo_ready, av_done = (
            sem("sc_done"), sem("af_ready"), sem("ahi_ready"), sem("alo_ready"), sem("av_done"))
        o1_ready, o2_ready, xo_ready = sem("o1_ready"), sem("o2_ready"), sem("xo_ready")
        up_done, gelu_done = sem("up_done"), sem("gelu_done")
        hsq_ready, hhi_ready, hlo_ready, hpart_ready = (
            sem("hsq_ready"), sem("hhi_ready"), sem("hlo_ready"), sem("hpart_ready"))
        hacc_ready = sem("hacc_ready")
        ss_turned, ss_ready, ss_root = sem("ss_turned"), sem("ss_ready"), sem("ss_root")
        hg_step = sem("hg_step")
        down_done, final_ready = sem("down_done"), sem("final_ready")
        LN_STEPS = 11

        def wait_if_any(engine, semaphore, value):
            if not isinstance(value, int) or value > 0:
                engine.wait_ge(semaphore, value)

        block = ctx.enter_context(nc.Block())

        @block.sync
        def _(sp):
            sp.dma_start(x_next[:], x_groups[0]).then_inc(x_loaded, 16)
            sp.dma_start(bias_rows[:], b_qkv.rearrange("(p n) -> p n", p=P)).then_inc(bias_rows_in, 16)
            for c in range(CC):
                sp.dma_start(pre["wqkv"][:, c], w_qkv[c * P:(c + 1) * P, :]).then_inc(wqkv_in[c], 16)
            sp.dma_start(bias[:].rearrange("p a b -> p (a b)"),
                         b_qkv.rearrange("(a n) -> a n", a=1).partition_broadcast(P)).then_inc(bias_in, 16)
            for c in range(4):
                sp.dma_start(pre["wup"][:, 4 * c:4 * c + 4],
                             w_up.rearrange("(f p) c -> p f c", p=P)[:, 4 * c:4 * c + 4]).then_inc(wup_in[c], 16)
            for c in range(CC):
                sp.dma_start(pre["wdn"][:, c], w_down[c * P:(c + 1) * P, :]).then_inc(wdn_in[c], 16)

            def group(s, more):
                if more:
                    sp.wait_ge(res_ready, 4 * s + 4)
                    sp.wait_ge(xf_ready, 4 * s + 4)
                    sp.dma_start(x_next[:], x_groups[s + 1]).then_inc(x_loaded, 16)
                for i in range(TILES):
                    sp.wait_ge(final_ready, 4 * s + i + 1)
                    sp.dma_start(out_tiles[s, i], xres[:, i]).then_inc(stored, 16)

            group(0, True)
            with sp.Fori(1, GROUPS - 1) as s:
                group(s, True)
            group(GROUPS - 1, False)
            sp.wait_ge(stored, 64 * GROUPS)

        @block.tensor
        def _(pe):
            def turn_weights(chunks):
                for n in range(4 * chunks.start, 4 * chunks.stop):
                    chunk, quarter = n // 4, n % 4
                    if quarter == 0:
                        pe.wait_ge(masks_ready, 2 * chunk + 2)
                    if n >= 4:
                        pe.wait_ge(wt_out, n - 3)
                    for m in range(4):
                        for k in range(2):
                            if chunk < 4:
                                src = pre[("up_pos", "up_neg")[k]][:, 4 * chunk + m, quarter * P:(quarter + 1) * P]
                            else:
                                f = 4 * quarter + m
                                src = pre[("dn_pos", "dn_neg")[k]][:, chunk - 4, f * P:(f + 1) * P]
                            last = pe.matmul(w_banks[n % 4][:, m * P:(m + 1) * P], src,
                                             (ident, minus_ident)[k][:], start=(k == 0), stop=(k == 1))
                    last.then_inc(wt_turned, 1)

            def turn_x(g, i, first=False):
                pe.wait_ge(xlo_ready, 4 * g + i + 1)
                if i >= 2:
                    pe.wait_ge(xT_ready, 4 * g + i - 1)
                elif not first:
                    pe.wait_ge(qkT_ready, 16 * g - 1 + i)
                for part in range(2):
                    for c in range(CC):
                        last = pe.transpose(tp[i % 2][:, (part * CC + c) * P:(part * CC + c + 1) * P],
                                            xs[:, i % 2, part, c * P:(c + 1) * P], ident[:])
                last.then_inc(x_turned, 1)

            def project(s, i, m, col):
                n = 3 * i + m
                if m == 0:
                    pe.wait_ge(xT_ready, 4 * s + i + 1)
                wait_if_any(pe, proj_out, 12 * s + max(n - 1, 0))
                k = 0
                for c in range(CC):
                    for part, wpart in ((0, 0), (0, 1), (1, 0)):
                        last = pe.matmul(proj[n % 2][:], xT[:, part, c, i * P:(i + 1) * P],
                                         wq16[:, wpart, c, col * C:(col + 1) * C],
                                         start=(k == 0), stop=(k == 3 * CC - 1))
                        k += 1
                last.then_inc(proj_done, 1)

            def up(s, f, begun):
                if f == 0:
                    pe.wait_ge(xT_ready, 4 * s + 4)
                if f < 2:
                    wait_if_any(pe, final_ready, 4 * s)
                    if begun:
                        pe.wait_ge(wt_out, 32)
                else:
                    pe.wait_ge(gelu_done, 16 * s + f - 1)
                for c in range(CC):
                    for part in range(2):
                        last = pe.matmul(ud[f % 2][:], wuT[:, c, f * P:(f + 1) * P], xT[:, part, c, :],
                                         start=(c == 0 and part == 0), stop=(c == CC - 1 and part == 1))
                last.then_inc(up_done, 1)

            def turn_qk(s, i, j):
                n = 4 * i + j
                pe.wait_ge(k_parts if j < 2 else q_parts, 4 * s + i + 1)
                if n >= 2:
                    pe.wait_ge(qkT_ready, 16 * s + n - 1)
                for m in range(8):
                    h = 8 * (j % 2) + m
                    src = (K16 if j < 2 else Q16)[:, h].rearrange("p a d -> p (a d)")
                    last = pe.transpose(tp[n % 2][:, m * P:(m + 1) * P], src, octets[:])
                last.then_inc(qk_turned, 1)

            def scores(s, i, j):
                n = 4 * i + j
                pe.wait_ge(qkT_ready, 16 * s + 4 * i + 4)
                wait_if_any(pe, af_ready, 16 * s + n)
                for m in range(4):
                    octet = slice(8 * (4 * j + m), 8 * (4 * j + m + 1))
                    last = pe.matmul(sc[:, m], KT[:, i % 2, octet].rearrange("p t h -> p (t h)"),
                                     QT[:, i % 2, octet].rearrange("p t h -> p (t h)"), start=True, stop=True)
                last.then_inc(sc_done, 1)

            def weigh(s, i, j):
                pe.wait_ge(alo_ready, 16 * s + 4 * i + j + 1)
                if j == 0:
                    pe.wait_ge(vlo_ready, 4 * s + i + 1)
                    wait_if_any(pe, o1_ready, 4 * s + i)
                for n in range(4 * j, 4 * j + 4):
                    k = 0
                    for a in (a_hi, a_lo):
                        for part in range(2):
                            last = pe.matmul(ov[:, n], a[:, n], V16[:, i, part, n * D:(n + 1) * D],
                                             start=(k == 0), stop=(k == 3))
                            k += 1
                last.then_inc(av_done, 1)

            def down(s, i, g):
                if i == 0:
                    if g == 0:
                        pe.wait_ge(gelu_done, 16 * s + 15)
                    pe.wait_ge(hlo_ready, 8 * s + g + 1)
                elif g == 0:
                    if i == 1:
                        pe.wait_ge(ss_ready, s + 1)
                    else:
                        pe.wait_ge(final_ready, 4 * s + i - 1)
                for f in (2 * g, 2 * g + 1):
                    for part in range(2):
                        last = pe.matmul(ud[i % 2][:], hT[:, part, f, i * P:(i + 1) * P], wdT[:, f, :],
                                         start=(f == 0 and part == 0), stop=(f == FC - 1 and part == 1))
                if g == PAIRS - 1:
                    last.then_inc(down_done, 1)

            def turn_sums(s):
                pe.wait_ge(gelu_done, 16 * s + 16)
                pe.wait_ge(hacc_ready, 7 * s + 7)
                for i in range(TILES):
                    last = pe.transpose(ud[1][:, i * P:(i + 1) * P], hacc[:, i * P:(i + 1) * P], ident32[:])
                last.then_inc(ss_turned, 1)

            def group(s, more, begun=False):
                for n in range(4):
                    def attend(turned=None, weighed=None, scored=None):
                        if weighed is not None and n >= 3:
                            weigh(s, n - 3, weighed)
                        if scored is not None and n >= 2:
                            scores(s, n - 2, scored)
                        if turned is not None and n >= 1:
                            turn_qk(s, n - 1, turned)
                    if n or not begun:
                        project(s, n, 0, 1)
                    attend(turned=0, weighed=0)
                    up(s, 4 * n, begun)
                    attend(turned=1, weighed=1, scored=0)
                    if n or not begun:
                        project(s, n, 1, 0)
                    attend(turned=2, weighed=2, scored=1)
                    up(s, 4 * n + 1, begun)
                    attend(turned=3, weighed=3)
                    project(s, n, 2, 2)
                    attend(scored=2)
                    up(s, 4 * n + 2, begun)
                    attend(scored=3)
                    up(s, 4 * n + 3, begun)
                fill = {
                    0: {0: [(turn_qk, 3, 0), (weigh, 1, 0)], 1: [(turn_qk, 3, 1), (weigh, 1, 1)],
                        2: [(scores, 2, 0), (turn_qk, 3, 2), (weigh, 1, 2)],
                        3: [(turn_qk, 3, 3), (weigh, 1, 3)], 4: [(scores, 2, 1)],
                        6: [(scores, 2, 2)], 7: [(scores, 2, 3)]},
                    1: {1: [(weigh, 2, 0), (scores, 3, 0)], 3: [(weigh, 2, 1), (scores, 3, 1)],
                        5: [(weigh, 2, 2), (scores, 3, 2)], 6: [(weigh, 2, 3)], 7: [(scores, 3, 3)]},
                    2: {3: [(weigh, 3, 0)], 4: [(weigh, 3, 1)], 5: [(weigh, 3, 2)], 6: [(weigh, 3, 3)]},
                    3: {}}
                turned = {(2, 1): 0, (2, 6): 1, (3, 2): 2, (3, 5): 3}
                for i in range(TILES):
                    for g in range(PAIRS):
                        down(s, i, g)
                        for piece, tile, j in fill[i].get(g, ()):
                            piece(s, tile, j)
                        if i == 0 and g == 5:
                            turn_sums(s)
                        if more and (i, g) in turned:
                            turn_x(s + 1, turned[i, g])

            pe.wait_ge(consts_made, 6)
            for i in range(TILES):
                turn_x(0, i, first=True)
            turn_weights(range(0, 4))
            pe.wait_ge(wq_lo_ready, CC)
            project(0, 0, 0, 1)
            turn_weights(range(4, 8))
            project(0, 0, 1, 0)
            group(0, True, begun=True)
            with pe.Fori(1, GROUPS - 1) as s:
                group(s, True)
            group(GROUPS - 1, False)

        @block.vector
        def _(dve):
            def weight_max(c):
                dve.wait_ge(wqkv_in[c], 16)
                dve.tensor_reduce(w_max[:, c:c + 1], pre["wqkv"][:, c], AX.X, ALU.max,
                                  apply_absolute_value=True).then_inc(max_done, 1)

            def bias_max():
                dve.wait_ge(bias_rows_in, 16)
                dve.tensor_reduce(b_max, bias_rows[:], AX.X, ALU.max,
                                  apply_absolute_value=True).then_inc(max_done, 1)

            def prepare():
                steps = [0]

                def then(ins):
                    steps[0] += 1
                    ins.then_inc(pre_step, 1)
                    dve.wait_ge(pre_step, steps[0])

                dve.wait_ge(abs_all, 1)
                then(dve.tensor_reduce(gmax, g_max, AX.X, ALU.max))
                then(dve.tensor_scalar(bound[:, 0:1], gmax, TINY, None, ALU.max))
                then(dve.scalar_tensor_tensor(out=bound[:, 1:2], in0=bound[:, 0:1], scalar=float(C),
                                              in1=g_bmax, op0=ALU.mult, op1=ALU.add))
                then(dve.tensor_scalar(pow2.bitcast(U32), bound.bitcast(U32), 0x7F800000, None, ALU.bitwise_and))
                then(dve.reciprocal(ipow2, pow2))
                dve.tensor_scalar(w_gain, ipow2[:, 0:1], TOP, None, ALU.mult)
                dve.tensor_scalar(w_unit, pow2[:, 0:1], 1.0 / (TOP * X_SCALE), None, ALU.mult)
                dve.tensor_scalar(qv_gain, ipow2[:, 1:2], TOP, None, ALU.mult)
                then(dve.tensor_scalar(o_unit, pow2[:, 1:2], 1.0 / TOP, None, ALU.mult))
                dve.tensor_tensor(v_mul, w_unit, qv_gain, ALU.mult)
                then(dve.tensor_scalar(qb_gain, qv_gain, SCALE, None, ALU.mult))
                dve.tensor_tensor(o_unit, o_unit, o_unit, ALU.mult)
                dve.wait_ge(bias_in, 16)
                dve.tensor_scalar(bias[:, 2], bias[:, 2], qv_gain, None, ALU.mult)
                dve.tensor_scalar(bias[:, 0], bias[:, 0], qb_gain, None, ALU.mult)
                dve.tensor_tensor(q_mul, w_unit, qb_gain, ALU.mult).then_inc(w_gain_ready, 1)
                dve.wait_ge(w_gain_ready, 1)

            def weight_lo(c):
                dve.wait_ge(wq_hi_ready, c + 1)
                dve.scalar_tensor_tensor(out=wq16[:, 1, c], in0=pre["wqkv"][:, c], scalar=w_gain,
                                         in1=wq16[:, 0, c], op0=ALU.mult, op1=ALU.subtract).then_inc(wq_lo_ready, 1)

            def up_sum(c):
                dve.wait_ge(wup_in[c], 16)
                dve.tensor_reduce(up_sums[:, c:c + 1], pre["wup"][:, 4 * c:4 * c + 4], AX.XY, ALU.add,
                                  apply_absolute_value=True).then_inc(up_sum_done, 1)

            def threshold(n):
                dve.wait_ge(abs_all, 2 + n)
                dve.tensor_reduce(gsum[:, n:n + 1], (g_up, g_dn)[n], AX.X, ALU.add).then_inc(pre_thr, 1)
                dve.wait_ge(pre_thr, 3 * n + 1)
                dve.tensor_scalar(thr[:, n:n + 1], gsum[:, n:n + 1], 0.5 / (FF * C), None, ALU.mult).then_inc(pre_thr, 1)
                dve.tensor_scalar(nthr[:, n:n + 1], gsum[:, n:n + 1], -0.5 / (FF * C), None,
                                  ALU.mult).then_inc(pre_thr, 1)
                dve.wait_ge(pre_thr, 3 * n + 3)

            def masks(n, c):
                rows = slice(4 * c, 4 * c + 4) if n == 0 else slice(c, c + 1)
                w, pos, neg = (pre[name][:, rows] for name in (("wup", "up_pos", "up_neg"), ("wdn", "dn_pos", "dn_neg"))[n])
                dve.tensor_scalar(pos, w, thr[:, n:n + 1], None, ALU.is_gt).then_inc(masks_ready, 1)
                dve.tensor_scalar(neg, w, nthr[:, n:n + 1], None, ALU.is_lt).then_inc(masks_ready, 1)

            def ln_stats(g, pair):
                dve.wait_ge(x_loaded, 16 * g + 16)
                for i in range(2 * pair, 2 * pair + 2):
                    dve.bn_stats(stats[:, i], x_next[:, i]).then_inc(ln_step, 1)

            def ln_var(g):
                dve.wait_ge(ln_step, LN_STEPS * g + 4)
                dve.tensor_tensor(m_sum, stats[:, :, 1], stats[:, :, 4], ALU.add)
                dve.tensor_tensor(m_diff, stats[:, :, 1], stats[:, :, 4], ALU.subtract)
                dve.tensor_tensor(v_sum, stats[:, :, 2], stats[:, :, 5], ALU.add).then_inc(ln_step, 1)
                dve.wait_ge(ln_step, LN_STEPS * g + 5)
                dve.tensor_scalar(mean, m_sum, 0.5, None, ALU.mult)
                dve.scalar_tensor_tensor(out=m_diff, in0=m_diff, scalar=0.25, in1=m_diff,
                                         op0=ALU.mult, op1=ALU.mult).then_inc(ln_step, 1)
                dve.wait_ge(ln_step, LN_STEPS * g + 6)
                dve.scalar_tensor_tensor(out=var2[:, TILES:], in0=v_sum, scalar=1.0 / C, in1=m_diff,
                                         op0=ALU.mult, op1=ALU.add).then_inc(ln_step, 1)
                dve.wait_ge(ln_step, LN_STEPS * g + 7)
                dve.tensor_scalar(var2[:, 0:TILES], var2[:, TILES:], LN_EPS, None, ALU.add).then_inc(ln_in, 1)

            def ln_scale(g):
                dve.wait_ge(ln_roots, g + 1)
                dve.reciprocal(inv_sd, root[:, 0:TILES]).then_inc(ln_step, 1)
                dve.wait_ge(ln_step, LN_STEPS * g + 8)
                dve.tensor_tensor(rms, root[:, TILES:], inv_sd, ALU.mult).then_inc(ln_step, 1)
                dve.wait_ge(ln_step, LN_STEPS * g + 9)
                dve.tensor_scalar(rms, rms, RMS_EPS, None, ALU.add).then_inc(ln_step, 1)
                dve.wait_ge(ln_step, LN_STEPS * g + 10)
                dve.reciprocal(inv_rms, rms).then_inc(ln_step, 1)
                dve.wait_ge(ln_step, LN_STEPS * g + 11)
                dve.scalar_tensor_tensor(out=x_gain, in0=inv_sd, scalar=X_SCALE, in1=inv_rms,
                                         op0=ALU.mult, op1=ALU.mult).then_inc(x_gain_ready, 1)

            def proj_gains(g):
                dve.tensor_scalar(q_gain, rms, q_mul, None, ALU.mult)
                dve.tensor_scalar(k_gain, rms, w_unit, None, ALU.mult)
                dve.tensor_scalar(v_gain, rms, v_mul, None, ALU.mult).then_inc(gains_ready, 1)

            def normalise(g, i):
                if i == 0:
                    dve.wait_ge(x_gain_ready, g + 1)
                wait_if_any(dve, xlo_ready, 4 * g + max(i - 1, 0))
                dve.tensor_scalar(xf[:, i % 2], x_next[:, i], mean[:, i:i + 1], x_gain[:, i:i + 1],
                                  ALU.subtract, ALU.mult).then_inc(xf_ready, 1)

            def proj_to(dst, s, i, m, col, gain):
                n = 3 * i + m
                dve.wait_ge(proj_done, 12 * s + n + 1)
                dve.scalar_tensor_tensor(out=dst, in0=proj[n % 2][:], scalar=gain[:, i:i + 1],
                                         in1=bias[:, col], op0=ALU.mult, op1=ALU.add).then_inc(proj_out, 1)

            def k_first(s, i):
                if i == 0:
                    dve.wait_ge(gains_ready, s + 1)
                wait_if_any(dve, klo_ready, 4 * s + i)
                proj_to(kr.rearrange("p h d -> p (h d)"), s, i, 0, 1, k_gain)
                dve.wait_ge(proj_out, 12 * s + 3 * i + 1)
                dve.tensor_reduce(kmax[:], kr, AX.X, ALU.max).then_inc(kmax_ready, 1)
                dve.wait_ge(kmax_ready, 4 * s + i + 1)
                dve.tensor_tensor(kr, kr, kmax[:].unsqueeze(2).broadcast_to([P, HEADS, D]),
                                  ALU.subtract).then_inc(kd_ready, 1)

            def k_sum(s, i):
                dve.wait_ge(ke_ready, 4 * s + i + 1)
                wait_if_any(dve, kn_ready, 4 * s + i)
                dve.tensor_reduce(ksum[:], kr, AX.X, ALU.add).then_inc(ks_ready, 1)
                dve.wait_ge(ks_ready, 8 * s + 2 * i + 1)
                dve.tensor_scalar(ksum[:], ksum[:], 1.0 / K_SCALE, None, ALU.mult).then_inc(ks_ready, 1)
                dve.wait_ge(ks_ready, 8 * s + 2 * i + 2)
                dve.reciprocal(kinv[:], ksum[:]).then_inc(kinv_ready, 1)

            def q_first(s, i):
                wait_if_any(dve, qlo_ready, 4 * s + i)
                proj_to(qr.rearrange("p h d -> p (h d)"), s, i, 1, 0, q_gain)

            def fill_k(s, i):
                dve.wait_ge(klo_ready, 4 * s + i + 1)
                dve.tensor_copy(K16[:, :, 3], K16[:, :, 2]).then_inc(k_parts, 1)

            def fill_q(s, i):
                dve.wait_ge(qlo_ready, 4 * s + i + 1)
                dve.tensor_copy(Q16[:, :, 3], Q16[:, :, 1]).then_inc(q_parts, 1)

            def v_first(s, i):
                wait_if_any(dve, vlo_ready, 4 * s + i)
                proj_to(vr, s, i, 2, 2, v_gain)
                dve.wait_ge(proj_out, 12 * s + 3 * i + 3)
                dve.transpose(v1, vr).then_inc(v1_ready, 1)
                dve.wait_ge(v1_ready, 4 * s + i + 1)
                dve.transpose(vr.rearrange("p (n a b) -> p n a b", n=OCT, a=2),
                              v1.rearrange("p (g n two) -> p n two g", g=HEADS, two=2)).then_inc(v2_ready, 1)

            def mask(s, i, j):
                n = 4 * i + j
                dve.wait_ge(sc_done, 16 * s + n + 1)
                wait_if_any(dve, alo_ready, 16 * s + max(n - 1, 0))
                dve.tensor_tensor(af[:, j % 2].rearrange("p (m n) -> p m n", m=4), sc[:],
                                  blocks[:].unsqueeze(1).broadcast_to([P, 4, P]),
                                  ALU.mult).then_inc(af_ready, 1)

            def h_parts(s, p):
                hp = hf[:, p % 2]
                dst = [hT[:, part, 2 * p:2 * p + 2].rearrange("p a b -> p (a b)") for part in range(2)]
                if p == 0:
                    wait_if_any(dve, down_done, 4 * s)
                dve.wait_ge(gelu_done, 16 * s + 2 * p + 2)
                dve.tensor_scalar(dst[0], hp, H_SCALE, None, ALU.mult).then_inc(hhi_ready, 1)
                dve.wait_ge(hhi_ready, 8 * s + p + 1)
                dve.scalar_tensor_tensor(out=dst[1], in0=hp, scalar=H_SCALE, in1=dst[0],
                                         op0=ALU.mult, op1=ALU.subtract).then_inc(hlo_ready, 1)

            def h_squares(s, p):
                dve.wait_ge(hsq_ready, 8 * s + p + 1)
                wait_if_any(dve, hacc_ready, 7 * s + (0 if p < 2 else max(p - 2, 1)))
                dve.tensor_tensor(hpart[:, p % 2], hsq[:, 0], hsq[:, 1], ALU.add).then_inc(hpart_ready, 1)

            def out_turn(s, i):
                dve.wait_ge(av_done, 16 * s + 4 * i + 4)
                dve.transpose(o1, ov[:].rearrange("p n d -> p (n d)")).then_inc(o1_ready, 1)
                dve.wait_ge(o1_ready, 4 * s + i + 1)
                dve.transpose(o2.rearrange("p (h d) -> p h d", h=HEADS),
                              o1.rearrange("p (t h) -> p h t", h=HEADS)).then_inc(o2_ready, 1)

            def add_x(s, i):
                dve.wait_ge(res_ready, 4 * s + i + 1)
                dve.wait_ge(o2_ready, 4 * s + i + 1)
                dve.scalar_tensor_tensor(out=xres[:, i], in0=o2, scalar=o_unit, in1=xres[:, i],
                                         op0=ALU.mult, op1=ALU.add).then_inc(xo_ready, 1)

            def sum_squares(s):
                dve.wait_ge(ss_turned, s + 1)
                dve.tensor_reduce(h_sum, ud[1][:].rearrange("p (i f) -> p i f", i=TILES), AX.X,
                                  ALU.add).then_inc(ss_ready, 1)

            def h_gains(s):
                dve.wait_ge(ss_root, s + 1)
                dve.tensor_scalar(h_root, h_root, float(FF) ** -0.5, RMS_EPS, ALU.mult, ALU.add).then_inc(hg_step, 1)
                dve.wait_ge(hg_step, 3 * s + 1)
                dve.reciprocal(h_gain, h_root).then_inc(hg_step, 1)
                dve.wait_ge(hg_step, 3 * s + 2)
                dve.tensor_scalar(h_gain, h_gain, 1.0 / H_SCALE, None, ALU.mult).then_inc(hg_step, 1)
                dve.wait_ge(hg_step, 3 * s + 3)

            def final(s, i):
                dve.wait_ge(down_done, 4 * s + i + 1)
                dve.wait_ge(xo_ready, 4 * s + i + 1)
                dve.scalar_tensor_tensor(out=xres[:, i], in0=ud[i % 2][:], scalar=h_gain[:, i:i + 1],
                                         in1=xres[:, i], op0=ALU.mult, op1=ALU.add).then_inc(final_ready, 1)

            def group(s, more):
                for n in range(4):
                    def mask_quarter(j):
                        if n >= 2:
                            mask(s, n - 2, j)
                    k_first(s, n)
                    mask_quarter(0)
                    k_sum(s, n)
                    mask_quarter(1)
                    q_first(s, n)
                    h_parts(s, 2 * n)
                    mask_quarter(2)
                    h_squares(s, 2 * n)
                    fill_k(s, n)
                    v_first(s, n)
                    mask_quarter(3)
                    fill_q(s, n)
                    if n == 3:
                        out_turn(s, 0)
                    h_parts(s, 2 * n + 1)
                    h_squares(s, 2 * n + 1)
                mask(s, 2, 0)
                add_x(s, 0)
                out_turn(s, 1)
                mask(s, 2, 1)
                if more:
                    ln_stats(s + 1, 0)
                sum_squares(s)
                mask(s, 2, 2)
                if more:
                    ln_stats(s + 1, 1)
                mask(s, 2, 3)
                if more:
                    ln_var(s + 1)
                mask(s, 3, 0)
                h_gains(s)
                final(s, 0)
                mask(s, 3, 1)
                add_x(s, 1)
                if more:
                    ln_scale(s + 1)
                    proj_gains(s + 1)
                    normalise(s + 1, 0)
                    normalise(s + 1, 1)
                mask(s, 3, 2)
                mask(s, 3, 3)
                final(s, 1)
                out_turn(s, 2)
                add_x(s, 2)
                if more:
                    normalise(s + 1, 2)
                    normalise(s + 1, 3)
                final(s, 2)
                out_turn(s, 3)
                add_x(s, 3)
                final(s, 3)

            ln_stats(0, 0)
            ln_stats(0, 1)
            ln_var(0)
            weight_max(0)
            ln_scale(0)
            normalise(0, 0)
            normalise(0, 1)
            weight_max(1)
            normalise(0, 2)
            weight_max(2)
            normalise(0, 3)
            weight_max(3)
            bias_max()
            prepare()
            proj_gains(0)
            up_sum(0)
            weight_lo(0)
            weight_lo(1)
            up_sum(2)
            weight_lo(2)
            threshold(0)
            for c in range(4):
                masks(0, c)
            weight_lo(3)
            threshold(1)
            for c in range(4):
                masks(1, c)
            dve.wait_ge(wt_turned, 32)
            group(0, True)
            with dve.Fori(1, GROUPS - 1) as s:
                group(s, True)
            group(GROUPS - 1, False)

        @block.scalar
        def _(act):
            def weight_sum(n, c):
                act.wait_ge((wup_in, wdn_in)[n][c], 16)
                if n == 0:
                    unread, w = pre["up_pos"][:, 4 * c:4 * c + 4], pre["wup"][:, 4 * c:4 * c + 4]
                else:
                    unread, w = pre["unread"][:, c % 3:c % 3 + 1], pre["wdn"][:, c:c + 1]
                    if c == 3:
                        act.wait_ge(dn_sum_done, 1)
                act.activation(unread.rearrange("p a b -> p (a b)"), w.rearrange("p a b -> p (a b)"), ACT.Abs,
                               accum_out=(up_sums, dn_sums)[n][:, c:c + 1]).then_inc((up_sum_done, dn_sum_done)[n], 1)

            def weight_hi(c):
                if c == 0:
                    act.wait_ge(w_gain_ready, 1)
                act.activation(wq16[:, 0, c], pre["wqkv"][:, c], ACT.Copy, scale=w_gain).then_inc(wq_hi_ready, 1)

            def weights_out(chunk):
                for n in range(4 * chunk, 4 * chunk + 4):
                    quarter = n % 4
                    act.wait_ge(wt_turned, n + 1)
                    bank = w_banks[n % 4]
                    if chunk < 4:
                        act.copy(wuT[:, quarter, chunk * 4 * P:(chunk + 1) * 4 * P], bank).then_inc(wt_out, 1)
                    else:
                        c = chunk - 4
                        act.copy(wdT[:, 4 * quarter:4 * quarter + 4, c * P:(c + 1) * P],
                                 bank.rearrange("p (m c) -> p m c", m=4)).then_inc(wt_out, 1)

            def x_hi(g, i):
                act.wait_ge(xf_ready, 4 * g + i + 1)
                wait_if_any(act, x_turned, 4 * g + max(i - 1, 0))
                act.copy(xs[:, i % 2, 0], xf[:, i % 2]).then_inc(xhi_ready, 1)

            def x_out(g, i):
                if i == 0:
                    wait_if_any(act, proj_done, 12 * g)
                    wait_if_any(act, up_done, 16 * g)
                act.wait_ge(x_turned, 4 * g + i + 1)
                act.copy(xT[:, :, :, i * P:(i + 1) * P],
                         tp[i % 2][:].rearrange("p (a c t) -> p a c t", a=2, c=CC)).then_inc(xT_ready, 1)

            def residual(s, i):
                if i == 0:
                    act.wait_ge(x_loaded, 16 * s + 16)
                    wait_if_any(act, stored, 64 * s)
                act.copy(xres[:, i], x_next[:, i]).then_inc(res_ready, 1)

            def qk_out(s, i, j):
                n = 4 * i + j
                if j == 0:
                    wait_if_any(act, sc_done, 16 * s + 4 * max(i - 1, 0))
                act.wait_ge(qk_turned, 16 * s + n + 1)
                dst = (KT if j < 2 else QT)[:, i % 2, :, 8 * (j % 2):8 * (j % 2) + 8]
                act.copy(dst, tp[n % 2][:].rearrange("p (h t) -> p t h", h=8)).then_inc(qkT_ready, 1)

            def gelu(s, f):
                p = f // 2
                wait_if_any(act, hlo_ready, 8 * s + max(p - 1, 0))
                act.wait_ge(up_done, 16 * s + f + 1)
                act.activation(hf[:, p % 2, (f % 2) * GT:(f % 2 + 1) * GT], ud[f % 2][:], ACT.Gelu,
                               scale=1.0 / X_SCALE).then_inc(gelu_done, 1)

            def square(s, p):
                act.wait_ge(gelu_done, 16 * s + 2 * p + 2)
                wait_if_any(act, hpart_ready, 8 * s + p)
                act.activation(hsq.rearrange("p a b -> p (a b)"), hf[:, p % 2], ACT.Square).then_inc(hsq_ready, 1)

            def q_hi(s, i):
                act.wait_ge(proj_out, 12 * s + 3 * i + 2)
                wait_if_any(act, qk_turned, 16 * s + 4 * i)
                act.copy(Q16[:, :, 0::2], qr.unsqueeze(2).broadcast_to([P, HEADS, 2, D])).then_inc(qhi_ready, 1)

            def k_exp(s, i):
                act.wait_ge(kd_ready, 4 * s + i + 1)
                act.activation(kr, kr, ACT.Exp).then_inc(ke_ready, 1)

            def k_hi(s, i):
                act.wait_ge(kn_ready, 4 * s + i + 1)
                wait_if_any(act, qk_turned, 16 * s + max(4 * i - 2, 0))
                act.copy(K16[:, :, 0:2], kr.unsqueeze(2).broadcast_to([P, HEADS, 2, D])).then_inc(khi_ready, 1)

            def v_hi(s, i):
                act.wait_ge(v2_ready, 4 * s + i + 1)
                wait_if_any(act, av_done, 16 * s)
                act.copy(V16[:, i, 0], vr).then_inc(vhi_ready, 1)

            def att_hi(s, i, j):
                n = 4 * i + j
                act.wait_ge(af_ready, 16 * s + n + 1)
                wait_if_any(act, av_done, 16 * s + max(n - 3, 0))
                act.copy(a_hi[:, 4 * j:4 * j + 4].rearrange("p a b -> p (a b)"), af[:, j % 2]).then_inc(ahi_ready, 1)

            def group(s, more):
                for n in range(4):
                    def turned(j):
                        if n >= 1:
                            qk_out(s, n - 1, j)

                    def weights(j):
                        if n >= 2:
                            att_hi(s, n - 2, j)
                    turned(0)
                    k_exp(s, n)
                    gelu(s, 4 * n)
                    turned(1)
                    weights(0)
                    turned(2)
                    weights(1)
                    k_hi(s, n)
                    gelu(s, 4 * n + 1)
                    square(s, 2 * n)
                    turned(3)
                    q_hi(s, n)
                    if n < 2:
                        residual(s, 2 * n)
                        residual(s, 2 * n + 1)
                    weights(2)
                    gelu(s, 4 * n + 2)
                    v_hi(s, n)
                    weights(3)
                    gelu(s, 4 * n + 3)
                    square(s, 2 * n + 1)
                for j in range(4):
                    qk_out(s, 3, j)
                    if j == 2:
                        att_hi(s, 2, 0)
                att_hi(s, 2, 1)
                att_hi(s, 2, 2)
                att_hi(s, 2, 3)
                att_hi(s, 3, 0)
                att_hi(s, 3, 1)
                if more:
                    x_hi(s + 1, 0)
                    x_hi(s + 1, 1)
                att_hi(s, 3, 2)
                att_hi(s, 3, 3)
                if more:
                    x_out(s + 1, 0)
                    x_hi(s + 1, 2)
                    x_out(s + 1, 1)
                    x_hi(s + 1, 3)
                    x_out(s + 1, 2)
                    x_out(s + 1, 3)

            x_hi(0, 0)
            x_hi(0, 1)
            x_out(0, 0)
            x_hi(0, 2)
            x_out(0, 1)
            x_hi(0, 3)
            x_out(0, 2)
            x_out(0, 3)
            weight_hi(0)
            weight_hi(1)
            weight_sum(0, 1)
            weight_hi(2)
            weight_sum(0, 3)
            weight_hi(3)
            weight_sum(1, 0)
            weight_sum(1, 1)
            weights_out(0)
            weight_sum(1, 2)
            weight_sum(1, 3)
            weights_out(1)
            weights_out(2)
            weights_out(3)
            for c in range(4):
                weights_out(4 + c)
            act.wait_ge(wq_lo_ready, CC)
            group(0, True)
            with act.Fori(1, GROUPS - 1) as s:
                group(s, True)
            group(GROUPS - 1, False)

        @block.gpsimd
        def _(pool):
            def prepare():
                pool.memset(ident32[:], 1.0).then_inc(consts_step, 1)
                pool.memset(ident[:], 1.0).then_inc(consts_step, 1)
                pool.memset(octets[:], 1.0).then_inc(consts_step, 1)
                pool.memset(minus_ident[:], -1.0).then_inc(consts_step, 1)
                pool.memset(blocks[:], 1.0 / K_SCALE).then_inc(consts_step, 1)
                pool.memset(half[:], 0.5).then_inc(consts_made, 1)
                pool.wait_ge(consts_step, 5)
                pool.affine_select(out=ident32[:], in_=ident32[:], compare_op=ALU.is_equal, fill=0.0, base=0,
                                   pattern=[[-1, P]], channel_multiplier=1).then_inc(consts_made, 1)
                pool.affine_select(out=ident[:], in_=ident[:], compare_op=ALU.is_equal, fill=0.0, base=0,
                                   pattern=[[-1, P]], channel_multiplier=1).then_inc(consts_made, 1)
                pool.affine_select(out=minus_ident[:], in_=minus_ident[:], compare_op=ALU.is_equal, fill=0.0, base=0,
                                   pattern=[[-1, P]], channel_multiplier=1).then_inc(consts_made, 1)
                o4 = octets[:].rearrange("p (n q two) -> p n q two", q=4, two=2)
                pool.affine_select(out=o4, in_=o4, compare_op=ALU.is_equal, fill=0.0, base=0,
                                   pattern=[[-2, OCT], [-32, 4], [-1, 2]],
                                   channel_multiplier=1).then_inc(consts_made, 1)
                b3 = blocks[:].rearrange("p (a b) -> p a b", b=HEADS)
                pool.affine_select(out=b3, in_=b3, compare_op=ALU.is_ge, fill=0.0, base=0,
                                   pattern=[[-HEADS, P // HEADS], [0, HEADS]],
                                   channel_multiplier=1).then_inc(consts_step, 1)
                pool.wait_ge(consts_step, 6)
                pool.affine_select(out=b3, in_=b3, compare_op=ALU.is_ge, fill=0.0, base=HEADS - 1,
                                   pattern=[[HEADS, P // HEADS], [0, HEADS]],
                                   channel_multiplier=-1).then_inc(consts_made, 1)

            def all_reduce(first, last, producer, value, op):
                pool.wait_ge(producer, value)
                pool.partition_all_reduce(g_parts[:, first:last], parts[:, first:last], P, op).then_inc(abs_all, 1)

            def ln_pow(g):
                pool.wait_ge(ln_in, g + 1)
                pool.tensor_tensor(root[:], var2[:], half[:], ALU.pow).then_inc(ln_roots, 1)

            def h_pow(s):
                pool.wait_ge(ss_ready, s + 1)
                pool.tensor_tensor(h_root, h_sum, half[:, 0:TILES], ALU.pow).then_inc(ss_root, 1)

            def x_lo(g, i):
                pool.wait_ge(xhi_ready, 4 * g + i + 1)
                pool.tensor_tensor(xs[:, i % 2, 1], xf[:, i % 2], xs[:, i % 2, 0],
                                   ALU.subtract).then_inc(xlo_ready, 1)

            def q_lo(s, i):
                pool.wait_ge(qhi_ready, 4 * s + i + 1)
                pool.tensor_tensor(Q16[:, :, 1], qr, Q16[:, :, 0], ALU.subtract).then_inc(qlo_ready, 1)

            def k_norm(s, i):
                pool.wait_ge(kinv_ready, 4 * s + i + 1)
                pool.tensor_tensor(kr, kr, kinv[:].unsqueeze(2).broadcast_to([P, HEADS, D]),
                                   ALU.mult).then_inc(kn_ready, 1)

            def k_lo(s, i):
                pool.wait_ge(khi_ready, 4 * s + i + 1)
                pool.tensor_tensor(K16[:, :, 2], kr, K16[:, :, 0], ALU.subtract).then_inc(klo_ready, 1)

            def v_lo(s, i):
                pool.wait_ge(vhi_ready, 4 * s + i + 1)
                pool.tensor_tensor(V16[:, i, 1], vr, V16[:, i, 0], ALU.subtract).then_inc(vlo_ready, 1)

            def att_lo(s, i, j):
                pool.wait_ge(ahi_ready, 16 * s + 4 * i + j + 1)
                pool.tensor_tensor(a_lo[:, 4 * j:4 * j + 4].rearrange("p a b -> p (a b)"), af[:, j % 2],
                                   a_hi[:, 4 * j:4 * j + 4].rearrange("p a b -> p (a b)"),
                                   ALU.subtract).then_inc(alo_ready, 1)

            def h_add(s, p):
                if p == 1:
                    wait_if_any(pool, ss_turned, s)
                else:
                    pool.wait_ge(hacc_ready, 7 * s + p - 1)
                pool.wait_ge(hpart_ready, 8 * s + p + 1)
                pool.tensor_tensor(hacc, hpart[:, 0] if p == 1 else hacc, hpart[:, p % 2],
                                   ALU.add).then_inc(hacc_ready, 1)

            def group(s, more):
                for n in range(4):
                    def weights(j):
                        if n >= 2:
                            att_lo(s, n - 2, j)
                    if n:
                        h_add(s, 2 * n - 1)
                    weights(0)
                    k_norm(s, n)
                    weights(1)
                    k_lo(s, n)
                    if n:
                        h_add(s, 2 * n)
                    q_lo(s, n)
                    weights(2)
                    v_lo(s, n)
                    weights(3)
                h_add(s, 7)
                for j in range(3):
                    att_lo(s, 2, j)
                h_pow(s)
                att_lo(s, 2, 3)
                if more:
                    ln_pow(s + 1)
                att_lo(s, 3, 0)
                att_lo(s, 3, 1)
                if more:
                    x_lo(s + 1, 0)
                    x_lo(s + 1, 1)
                att_lo(s, 3, 2)
                att_lo(s, 3, 3)
                if more:
                    x_lo(s + 1, 2)
                    x_lo(s + 1, 3)

            prepare()
            ln_pow(0)
            for i in range(TILES):
                x_lo(0, i)
            all_reduce(0, 5, max_done, 5, bass.bass_isa.ReduceOp.max)
            all_reduce(5, 9, up_sum_done, 4, bass.bass_isa.ReduceOp.add)
            all_reduce(9, 13, dn_sum_done, 4, bass.bass_isa.ReduceOp.add)
            pool.wait_ge(wt_turned, 32)
            pool.wait_ge(wq_lo_ready, CC)
            group(0, True)
            with pool.Fori(1, GROUPS - 1) as s:
                group(s, True)
            group(GROUPS - 1, False)


_INS = ['L0_attn_x', 'L0_attn_W_qkv', 'L0_attn_b_qkv', 'L0_ffn_w_up', 'L0_ffn_w_down']
_OUTS = [((8, 1024, 512), 'float32')]


def kernel(**inputs):
    import numpy as _np
    import concourse.bacc as _bacc
    from concourse import mybir as _mybir
    from concourse.bass_utils import run_bass_kernel_spmd as _run

    nc = _bacc.Bacc("TRN2", target_bir_lowering=False, num_devices=1)
    arrays, args = {}, []
    for name in _INS:
        a = _np.ascontiguousarray(inputs[name])
        arrays[f"in_{name}_dram"] = a
        args.append(nc.dram_tensor(f"in_{name}_dram", a.shape, _mybir.dt.from_np(a.dtype), kind="ExternalInput").ap())
    for i, (shape, dtype) in enumerate(_OUTS):
        dt = _mybir.dt.from_np(_np.dtype(dtype))
        args.append(nc.dram_tensor(f"out_{i}_dram", shape, dt, kind="ExternalOutput").ap())
    layer_kernel(nc, *args)
    r = _run(nc, [arrays], core_ids=[0])
    return r.results[0]["out_0_dram"]
```

```python
from contextlib import ExitStack

import numpy as np

import concourse.bass as bass
from concourse import mybir

ALU = mybir.AluOpType
ACT = mybir.ActivationFunctionType
AX = mybir.AxisListType
F32 = mybir.dt.float32
F16 = mybir.dt.float16
U32 = mybir.dt.uint32

P = 128
HEADS = 16
X_SCALE = 2.0 ** 10
H_SCALE = 2.0 ** 6
K_SCALE = 2.0 ** 14
TOP = 2.0 ** 14
LN_EPS = 1e-5
RMS_EPS = 1e-8
TINY = 1e-30


def carve(region, sizes):
    out, at = {}, 0
    for name, (shape, dt) in sizes.items():
        words = int(np.prod(shape)) * (2 if dt == F16 else 4) // 4
        v = region[:, at:at + words]
        if dt != F32:
            v = v.bitcast(dt)
        if len(shape) == 2:
            v = v.rearrange("p (a b) -> p a b", a=shape[0])
        if len(shape) == 3:
            v = v.rearrange("p (a b c) -> p a b c", a=shape[0], b=shape[1])
        out[name] = v
        at += words
    assert at <= region.shape[1], (at, region.shape)
    return out


def layer_kernel(nc, x, w_qkv, b_qkv, w_up, w_down, out):
    batch, seq, C = x.shape
    TOKENS = batch * seq
    FF = w_up.shape[0]
    D = C // HEADS
    SCALE = float(D) ** -0.5
    TILES = 4
    GT = TILES * P
    GROUPS = TOKENS // GT
    CC = C // P
    FC = FF // P
    PAIRS = FC // 2
    PAIRED = HEADS // 2
    OCT = P // 8
    assert C == 512 and D == 32 and FC == 16 and CC == 4

    x_groups = x.rearrange("a b c -> (a b) c").rearrange("(s i p) c -> s p i c", i=TILES, p=P)
    out_tiles = out.rearrange("a b c -> (a b) c").rearrange("(s i p) c -> s i p c", i=TILES, p=P)

    with ExitStack() as ctx:
        def sb(name, shape, dt):
            return ctx.enter_context(nc.sbuf_tensor(name, shape, dt))

        def psum(name, shape, dt):
            return ctx.enter_context(nc.psum_tensor(name, shape, dt))

        def sem(name):
            return ctx.enter_context(nc.semaphore(name))

        wq16 = sb("wq16", [P, 2, CC, 3 * C], F16)
        wuT = sb("wuT", [P, CC, FF], F16)
        wdT = sb("wdT", [P, FC, C], F16)
        bias = sb("bias", [P, 3, C], F32)
        ident = sb("ident", [P, P], F16)
        minus_ident = sb("minus_ident", [P, P], F16)
        order = sb("order", [P, P], F16)
        ident32 = sb("ident32", [P, P], F32)
        blocks = sb("blocks", [P, P], F32)
        parity = sb("parity", [P, 2], F32)
        half = sb("half", [P, 2 * TILES], F32)
        cst = sb("cst", [P, 24], F32)
        bias_rows = sb("bias_rows", [P, 3 * C // P], F32)
        parts = sb("parts", [P, 16], F32)
        g_parts = sb("g_parts", [P, 16], F32)
        x_next = sb("x_next", [P, TILES, C], F32)
        xf = sb("xf", [P, 2, C], F32)
        xs = sb("xs", [P, 2, 2, C], F16)
        xT = sb("xT", [P, 2, CC, GT], F16)
        stats = sb("stats", [P, TILES, 6], F32)
        mv = sb("mv", [P, 4, TILES], F32)
        var2 = sb("var2", [P, 2 * TILES], F32)
        root = sb("root", [P, 2 * TILES], F32)
        ln = sb("ln", [P, 8, TILES], F32)
        hn = sb("hn", [P, 4, TILES], F32)
        inv_sd, rms, inv_rms, x_gain, q_gain, k_gain, v_gain = (ln[:, n, :] for n in range(7))
        mean, m_sum, m_diff, v_sum = (mv[:, n] for n in range(4))
        h_sum, h_root, h_gain = (hn[:, n, :] for n in range(3))
        kmax = sb("kmax", [P, HEADS], F32)
        ksum = sb("ksum", [P, HEADS], F32)
        kinv = sb("kinv", [P, HEADS], F32)

        region = sb("region", [P, 118 * 256], F32)
        pre = carve(region, {
            "wqkv": ((CC, 3 * C), F32), "wup": ((FC, C), F32), "wdn": ((CC, FF), F32),
            "up_pos": ((FC, C), F16), "unread": ((3, FF), F16)})
        wup_at = CC * 3 * C
        pre.update(carve(region[:, wup_at:wup_at + FC * C], {"dn_pos": ((CC, FF), F16), "dn_neg": ((CC, FF), F16)}))
        pre["up_neg"] = wdT
        work = carve(region, {
            "hT": ((2, FC, GT), F16), "hf": ((2, 2 * GT), F32), "hsq": ((2, GT), F32),
            "hpart": ((2, GT), F32), "hacc": ((GT,), F32), "xres": ((TILES, C), F32),
            "KT": ((2, P * HEADS), F16), "QT": ((2, P * HEADS), F16), "rows": ((2, P * PAIRED), F16),
            "V16": ((TILES, 2, C), F16), "af": ((2, C), F32), "a_hi": ((OCT, P), F16),
            "a_lo": ((OCT, P), F16), "kr": ((HEADS, D), F32), "qr": ((HEADS, D), F32),
            "vr": ((C,), F32), "v1": ((C,), F32), "o0": ((OCT, 2, D), F32), "o1": ((C,), F32), "o2": ((C,), F32),
            "K16": ((PAIRED, 2, 2 * D), F16), "Q16": ((PAIRED, 2, 2 * D), F16)})
        hT, hf, hsq, hpart, hacc, xres = (work[n] for n in ("hT", "hf", "hsq", "hpart", "hacc", "xres"))
        KT, QT, V16, af, a_hi, a_lo = (work[n] for n in ("KT", "QT", "V16", "af", "a_hi", "a_lo"))
        kr, qr, vr, v1, o0, o1, o2, K16, Q16, rows = (
            work[n] for n in ("kr", "qr", "vr", "v1", "o0", "o1", "o2", "K16", "Q16", "rows"))

        def heads(t):
            return t.rearrange("p (a m) d -> p a m d", a=2)

        def part16(t, part):
            return t.rearrange("p m a (r d) -> p a m r d", r=2)[:, :, :, part]

        proj = [psum(f"proj{n}", [P, C], F32) for n in range(2)]
        ud = [psum(f"ud{n}", [P, GT], F32) for n in range(2)]
        tp = [psum(f"tp{n}", [P, 2 * GT], F16) for n in range(2)]
        sc = psum("sc", [P, 4, P], F32)
        ov = psum("ov", [P, OCT // 2, 2, D], F32)

        w_banks = [tp[0][:].bitcast(F32), tp[1][:].bitcast(F32), sc[:].rearrange("p a b -> p (a b)"),
                   ov[:].rearrange("p n r d -> p (n r d)")]

        w_max, b_max, up_sums, dn_sums = parts[:, 0:CC], parts[:, CC:CC + 1], parts[:, 5:9], parts[:, 9:13]
        g_max, g_bmax, g_up, g_dn = g_parts[:, 0:CC], g_parts[:, CC:CC + 1], g_parts[:, 5:9], g_parts[:, 9:13]
        gmax = cst[:, 0:1]
        gsum = cst[:, 2:4]
        thr = cst[:, 8:10]
        nthr = cst[:, 10:12]
        bound = cst[:, 12:14]
        pow2 = cst[:, 14:16]
        ipow2 = cst[:, 16:18]
        w_gain, w_unit, qv_gain, q_mul, v_mul, o_unit = (cst[:, n:n + 1] for n in range(18, 24))
        qb_gain = ln[:, 7, 0:1]

        bias_in, bias_rows_in = sem("bias_in"), sem("bias_rows_in")
        wqkv_in = [sem(f"wqkv_in{c}") for c in range(CC)]
        wup_in = [sem(f"wup_in{c}") for c in range(4)]
        wdn_in = [sem(f"wdn_in{c}") for c in range(CC)]
        consts_made = sem("consts_made")
        max_done = sem("max_done")
        up_sum_done, dn_sum_done = sem("up_sum_done"), sem("dn_sum_done")
        consts_step, pre_thr = sem("consts_step"), sem("pre_thr")
        w_gain_ready = sem("w_gain_ready")
        abs_all = sem("abs_all")
        pre_step = sem("pre_step")
        x_gain_ready, gains_ready = sem("x_gain_ready"), sem("gains_ready")
        wq_hi_ready, wq_lo_ready = sem("wq_hi_ready"), sem("wq_lo_ready")
        masks_ready = sem("masks_ready")
        wt_turned = sem("wt_turned")
        wt_out = sem("wt_out")
        x_loaded = sem("x_loaded")
        stored = sem("stored")
        ln_step = sem("ln_step")
        ln_roots = sem("ln_roots")
        ln_in = sem("ln_in")
        xf_ready, xhi_ready, xlo_ready = sem("xf_ready"), sem("xhi_ready"), sem("xlo_ready")
        x_turned, xT_ready, res_ready = sem("x_turned"), sem("xT_ready"), sem("res_ready")
        proj_done, proj_out = sem("proj_done"), sem("proj_out")
        kmax_ready, kd_ready, ke_ready, ks_ready = sem("kmax_ready"), sem("kd_ready"), sem("ke_ready"), sem("ks_ready")
        kinv_ready, kn_ready, khi_ready, klo_ready = sem("kinv_ready"), sem("kn_ready"), sem("khi_ready"), sem("klo_ready")
        qhi_ready, qlo_ready = sem("qhi_ready"), sem("qlo_ready")
        v1_ready, v2_ready, vhi_ready, vlo_ready = sem("v1_ready"), sem("v2_ready"), sem("vhi_ready"), sem("vlo_ready")
        blocks_ready = sem("blocks_ready")
        qk_turned, rows_out = sem("qk_turned"), sem("rows_out")
        kT_in, qT_in = [sem(f"kT_in{r}") for r in range(2)], [sem(f"qT_in{r}") for r in range(2)]
        sc_done, af_ready, ahi_ready, alo_ready, av_done = (
            sem("sc_done"), sem("af_ready"), sem("ahi_ready"), sem("alo_ready"), sem("av_done"))
        ov_out, o0_ready = sem("ov_out"), sem("o0_ready")
        o1_ready, o2_ready, xo_ready = sem("o1_ready"), sem("o2_ready"), sem("xo_ready")
        up_done, gelu_done = sem("up_done"), sem("gelu_done")
        hsq_ready, hhi_ready, hlo_ready, hpart_ready = (
            sem("hsq_ready"), sem("hhi_ready"), sem("hlo_ready"), sem("hpart_ready"))
        hacc_ready = sem("hacc_ready")
        ss_turned, ss_ready, ss_root = sem("ss_turned"), sem("ss_ready"), sem("ss_root")
        hg_step = sem("hg_step")
        down_done, final_ready = sem("down_done"), sem("final_ready")
        LN_STEPS = 11

        def wait_if_any(engine, semaphore, value):
            if not isinstance(value, int) or value > 0:
                engine.wait_ge(semaphore, value)

        block = ctx.enter_context(nc.Block())

        @block.sync
        def _(sp):
            sp.dma_start(x_next[:], x_groups[0]).then_inc(x_loaded, 16)
            sp.dma_start(bias_rows[:], b_qkv.rearrange("(p n) -> p n", p=P)).then_inc(bias_rows_in, 16)
            for c in range(CC):
                sp.dma_start(pre["wqkv"][:, c], w_qkv[c * P:(c + 1) * P, :]).then_inc(wqkv_in[c], 16)
            sp.dma_start(bias[:].rearrange("p a b -> p (a b)"),
                         b_qkv.rearrange("(a n) -> a n", a=1).partition_broadcast(P)).then_inc(bias_in, 16)
            for c in range(4):
                sp.dma_start(pre["wup"][:, 4 * c:4 * c + 4],
                             w_up.rearrange("(f p) c -> p f c", p=P)[:, 4 * c:4 * c + 4]).then_inc(wup_in[c], 16)
            for c in range(CC):
                sp.dma_start(pre["wdn"][:, c], w_down[c * P:(c + 1) * P, :]).then_inc(wdn_in[c], 16)

            def spread_k(s, i):
                sp.wait_ge(rows_out, 8 * s + 2 * i + 1)
                src = rows[:, 0].rearrange("p (x n) -> p x n", x=8)
                dst = KT[:, i % 2].rearrange("p (x a n) -> p a x n", x=8, a=2)
                for a in range(2):
                    for row in (0, 2 * D):
                        sp.dma_start(dst[row:row + 2 * D, a], src[2 * D * a:2 * D * (a + 1)]).then_inc(kT_in[i % 2], 16)

            def spread_q(s, i):
                sp.wait_ge(rows_out, 8 * s + 2 * i + 2)
                src = rows[:, 1].rearrange("p (x n) -> p x n", x=8)
                dst = QT[:, i % 2].rearrange("p (x a n) -> p a x n", x=8, a=2)
                for a in range(2):
                    at = 2 * D * a
                    sp.dma_start(dst[0:2 * D, a], src[at:at + 2 * D]).then_inc(qT_in[i % 2], 16)
                    sp.dma_start(dst[2 * D:3 * D, a], src[at + D:at + 2 * D]).then_inc(qT_in[i % 2], 16)
                    sp.dma_start(dst[3 * D:4 * D, a], src[at:at + D]).then_inc(qT_in[i % 2], 16)

            def group(s, more):
                spread_k(s, 0)
                spread_q(s, 0)
                if more:
                    sp.wait_ge(res_ready, 4 * s + 4)
                    sp.wait_ge(xf_ready, 4 * s + 4)
                    sp.dma_start(x_next[:], x_groups[s + 1]).then_inc(x_loaded, 16)
                for i in range(1, TILES):
                    spread_k(s, i)
                    spread_q(s, i)
                for i in range(TILES):
                    sp.wait_ge(final_ready, 4 * s + i + 1)
                    sp.dma_start(out_tiles[s, i], xres[:, i]).then_inc(stored, 16)

            group(0, True)
            with sp.Fori(1, GROUPS - 1) as s:
                group(s, True)
            group(GROUPS - 1, False)
            sp.wait_ge(stored, 64 * GROUPS)

        @block.tensor
        def _(pe):
            def turn_weights(chunks):
                for n in range(4 * chunks.start, 4 * chunks.stop):
                    chunk, quarter = n // 4, n % 4
                    if quarter == 0:
                        pe.wait_ge(masks_ready, 2 * chunk + 2)
                    if n >= 4:
                        pe.wait_ge(wt_out, n - 3)
                    for m in range(4):
                        for k in range(2):
                            if chunk < 4:
                                src = pre[("up_pos", "up_neg")[k]][:, 4 * chunk + m, quarter * P:(quarter + 1) * P]
                            else:
                                f = 4 * quarter + m
                                src = pre[("dn_pos", "dn_neg")[k]][:, chunk - 4, f * P:(f + 1) * P]
                            last = pe.matmul(w_banks[n % 4][:, m * P:(m + 1) * P], src,
                                             (ident, minus_ident)[k][:], start=(k == 0), stop=(k == 1))
                    last.then_inc(wt_turned, 1)

            def turn_x(g, i, first=False):
                pe.wait_ge(xlo_ready, 4 * g + i + 1)
                if i >= 2:
                    pe.wait_ge(xT_ready, 4 * g + i - 1)
                elif not first:
                    pe.wait_ge(rows_out, 8 * g - 1 + i)
                for part in range(2):
                    for c in range(CC):
                        last = pe.transpose(tp[i % 2][:, (part * CC + c) * P:(part * CC + c + 1) * P],
                                            xs[:, i % 2, part, c * P:(c + 1) * P], ident[:])
                last.then_inc(x_turned, 1)

            def project(s, i, m, col):
                n = 3 * i + m
                if m == 0:
                    pe.wait_ge(xT_ready, 4 * s + i + 1)
                wait_if_any(pe, proj_out, 12 * s + max(n - 1, 0))
                k = 0
                for c in range(CC):
                    for part, wpart in ((0, 0), (0, 1), (1, 0)):
                        last = pe.matmul(proj[n % 2][:], xT[:, part, c, i * P:(i + 1) * P],
                                         wq16[:, wpart, c, col * C:(col + 1) * C],
                                         start=(k == 0), stop=(k == 3 * CC - 1))
                        k += 1
                last.then_inc(proj_done, 1)

            def up(s, f, begun=False):
                if f == 0:
                    pe.wait_ge(xT_ready, 4 * s + 4)
                if f < 2:
                    wait_if_any(pe, final_ready, 4 * s)
                    if begun:
                        pe.wait_ge(wt_out, 16)
                else:
                    pe.wait_ge(gelu_done, 16 * s + f - 1)
                for c in range(CC):
                    for part in range(2):
                        last = pe.matmul(ud[f % 2][:], wuT[:, c, f * P:(f + 1) * P], xT[:, part, c, :],
                                         start=(c == 0 and part == 0), stop=(c == CC - 1 and part == 1))
                last.then_inc(up_done, 1)

            def turn_qk(s, i, j):
                n = 2 * i + j
                pe.wait_ge((klo_ready, qlo_ready)[j], 4 * s + i + 1)
                if n >= 2:
                    pe.wait_ge(rows_out, 8 * s + n - 1)
                for m in range(PAIRED):
                    src = (K16, Q16)[j][:, m].rearrange("p a n -> p (a n)")
                    last = pe.transpose(tp[j][:, m * P:(m + 1) * P], src, order[:])
                last.then_inc(qk_turned, 1)

            def scores(s, i, j):
                n = 4 * i + j
                if j == 0:
                    pe.wait_ge(kT_in[i % 2], 128 * s + 64 * (i // 2) + 64)
                    pe.wait_ge(qT_in[i % 2], 192 * s + 96 * (i // 2) + 96)
                wait_if_any(pe, af_ready, 16 * s + n)
                k_oct, q_oct = (t[:, i % 2].rearrange("p (i c l) -> p i l c", i=2, l=8)[:, j // 2] for t in (KT, QT))
                for m in range(4):
                    last = pe.matmul(sc[:, m], k_oct[:, 4 * (j % 2) + m], q_oct[:, 4 * (j % 2) + m], start=True, stop=True)
                last.then_inc(sc_done, 1)

            def weigh(s, i, j):
                pe.wait_ge(alo_ready, 16 * s + 4 * i + j + 1)
                if j == 0:
                    pe.wait_ge(vlo_ready, 4 * s + i + 1)
                if j % 2 == 0:
                    wait_if_any(pe, ov_out, 8 * s + 2 * i + j // 2)
                for n in range(4 * j, 4 * j + 4):
                    for k, a in enumerate((a_hi, a_lo)):
                        last = pe.matmul(ov[:, n % 8], a[:, n], V16[:, i, :, n * D:(n + 1) * D],
                                         start=(k == 0), stop=(k == 1))
                last.then_inc(av_done, 1)

            def down(s, i, g):
                if i == 0:
                    if g == 0:
                        pe.wait_ge(gelu_done, 16 * s + 15)
                    pe.wait_ge(hlo_ready, 8 * s + g + 1)
                elif g == 0:
                    if i == 1:
                        pe.wait_ge(ss_ready, s + 1)
                    else:
                        pe.wait_ge(final_ready, 4 * s + i - 1)
                for f in (2 * g, 2 * g + 1):
                    for part in range(2):
                        last = pe.matmul(ud[i % 2][:], hT[:, part, f, i * P:(i + 1) * P], wdT[:, f, :],
                                         start=(f == 0 and part == 0), stop=(f == FC - 1 and part == 1))
                if g == PAIRS - 1:
                    last.then_inc(down_done, 1)

            def turn_sums(s):
                pe.wait_ge(gelu_done, 16 * s + 16)
                pe.wait_ge(hacc_ready, 7 * s + 7)
                for i in range(TILES):
                    last = pe.transpose(ud[1][:, i * P:(i + 1) * P], hacc[:, i * P:(i + 1) * P], ident32[:])
                last.then_inc(ss_turned, 1)

            def group(s, more, begun=False):
                for n in range(4):
                    def attend(turned=None, weighed=None, scored=None):
                        if weighed is not None and n >= 3:
                            weigh(s, n - 3, weighed)
                        if scored is not None and n >= 2:
                            scores(s, n - 2, scored)
                        if turned is not None and n >= 1:
                            turn_qk(s, n - 1, turned)
                    if begun and n == 1:
                        pe.wait_ge(wt_out, 32)
                    if n or not begun:
                        project(s, n, 0, 1)
                    attend(turned=0, weighed=0)
                    if n or not begun:
                        up(s, 4 * n)
                    attend(weighed=1, scored=0)
                    if n or not begun:
                        project(s, n, 1, 0)
                    attend(turned=1, weighed=2, scored=1)
                    if n or not begun:
                        up(s, 4 * n + 1)
                    attend(weighed=3)
                    project(s, n, 2, 2)
                    attend(scored=2)
                    up(s, 4 * n + 2)
                    attend(scored=3)
                    up(s, 4 * n + 3)
                fill = {
                    0: {0: [(turn_qk, 3, 0), (weigh, 1, 0)], 1: [(weigh, 1, 1)],
                        2: [(scores, 2, 0), (turn_qk, 3, 1)],
                        4: [(weigh, 1, 2), (scores, 2, 1)], 5: [(weigh, 1, 3)],
                        6: [(scores, 2, 2)], 7: [(scores, 2, 3)]},
                    1: {1: [(weigh, 2, 0)], 2: [(scores, 3, 0)], 3: [(weigh, 2, 1)], 4: [(scores, 3, 1)],
                        5: [(weigh, 2, 2), (scores, 3, 2)], 6: [(weigh, 2, 3)]},
                    2: {0: [(scores, 3, 3)], 3: [(weigh, 3, 0)], 4: [(weigh, 3, 1)], 6: [(weigh, 3, 2)], 7: [(weigh, 3, 3)]},
                    3: {}}
                turned = {(2, 1): 0, (2, 6): 1, (3, 2): 2, (3, 5): 3}
                for i in range(TILES):
                    for g in range(PAIRS):
                        down(s, i, g)
                        for piece, tile, j in fill[i].get(g, ()):
                            piece(s, tile, j)
                        if i == 0 and g == 5:
                            turn_sums(s)
                        if more and (i, g) in turned:
                            turn_x(s + 1, turned[i, g])

            pe.wait_ge(consts_made, 7)
            for i in range(TILES):
                turn_x(0, i, first=True)
            pe.wait_ge(xT_ready, TILES)
            pe.wait_ge(wq_lo_ready, CC)
            project(0, 0, 0, 1)
            turn_weights(range(0, 1))
            project(0, 0, 1, 0)
            turn_weights(range(1, 5))
            up(0, 0, begun=True)
            turn_weights(range(5, 6))
            up(0, 1, begun=True)
            turn_weights(range(6, 8))
            group(0, True, begun=True)
            with pe.Fori(1, GROUPS - 1) as s:
                group(s, True)
            group(GROUPS - 1, False)

        @block.vector
        def _(dve):
            def own_token():
                dve.wait_ge(consts_made, 7)
                dve.tensor_reduce(parity[:], ident32[:].rearrange("p (a u) -> p u a", u=2), AX.X,
                                  ALU.add).then_inc(blocks_ready, 1)
                dve.wait_ge(blocks_ready, 1)
                b3 = blocks[:].rearrange("p (a u) -> p a u", u=2)
                dve.tensor_tensor(b3, b3, parity[:].unsqueeze(1).broadcast_to([P, P // 2, 2]),
                                  ALU.mult).then_inc(blocks_ready, 1)
                dve.wait_ge(blocks_ready, 2)

            def weight_max(c):
                dve.wait_ge(wqkv_in[c], 16)
                dve.tensor_reduce(w_max[:, c:c + 1], pre["wqkv"][:, c], AX.X, ALU.max,
                                  apply_absolute_value=True).then_inc(max_done, 1)

            def bias_max():
                dve.wait_ge(bias_rows_in, 16)
                dve.tensor_reduce(b_max, bias_rows[:], AX.X, ALU.max,
                                  apply_absolute_value=True).then_inc(max_done, 1)

            def prepare():
                steps = [0]

                def then(ins):
                    steps[0] += 1
                    ins.then_inc(pre_step, 1)
                    dve.wait_ge(pre_step, steps[0])

                dve.wait_ge(abs_all, 1)
                then(dve.tensor_reduce(gmax, g_max, AX.X, ALU.max))
                then(dve.tensor_scalar(bound[:, 0:1], gmax, TINY, None, ALU.max))
                then(dve.scalar_tensor_tensor(out=bound[:, 1:2], in0=bound[:, 0:1], scalar=float(C),
                                              in1=g_bmax, op0=ALU.mult, op1=ALU.add))
                then(dve.tensor_scalar(pow2.bitcast(U32), bound.bitcast(U32), 0x7F800000, None, ALU.bitwise_and))
                then(dve.reciprocal(ipow2, pow2))
                dve.tensor_scalar(w_gain, ipow2[:, 0:1], TOP, None, ALU.mult)
                dve.tensor_scalar(w_unit, pow2[:, 0:1], 1.0 / (TOP * X_SCALE), None, ALU.mult)
                dve.tensor_scalar(qv_gain, ipow2[:, 1:2], TOP, None, ALU.mult)
                then(dve.tensor_scalar(o_unit, pow2[:, 1:2], 1.0 / TOP, None, ALU.mult))
                dve.tensor_tensor(v_mul, w_unit, qv_gain, ALU.mult)
                then(dve.tensor_scalar(qb_gain, qv_gain, SCALE, None, ALU.mult))
                dve.tensor_tensor(o_unit, o_unit, o_unit, ALU.mult)
                dve.wait_ge(bias_in, 16)
                dve.tensor_scalar(bias[:, 2], bias[:, 2], qv_gain, None, ALU.mult)
                dve.tensor_scalar(bias[:, 0], bias[:, 0], qb_gain, None, ALU.mult)
                dve.tensor_tensor(q_mul, w_unit, qb_gain, ALU.mult).then_inc(w_gain_ready, 1)
                dve.wait_ge(w_gain_ready, 1)

            def weight_lo(c):
                dve.wait_ge(wq_hi_ready, c + 1)
                dve.scalar_tensor_tensor(out=wq16[:, 1, c], in0=pre["wqkv"][:, c], scalar=w_gain,
                                         in1=wq16[:, 0, c], op0=ALU.mult, op1=ALU.subtract).then_inc(wq_lo_ready, 1)

            def up_sum(c):
                dve.wait_ge(wup_in[c], 16)
                dve.tensor_reduce(up_sums[:, c:c + 1], pre["wup"][:, 4 * c:4 * c + 4], AX.XY, ALU.add,
                                  apply_absolute_value=True).then_inc(up_sum_done, 1)

            def threshold(n):
                dve.wait_ge(abs_all, 2 + n)
                dve.tensor_reduce(gsum[:, n:n + 1], (g_up, g_dn)[n], AX.X, ALU.add).then_inc(pre_thr, 1)
                dve.wait_ge(pre_thr, 3 * n + 1)
                dve.tensor_scalar(thr[:, n:n + 1], gsum[:, n:n + 1], 0.5 / (FF * C), None, ALU.mult).then_inc(pre_thr, 1)
                dve.tensor_scalar(nthr[:, n:n + 1], gsum[:, n:n + 1], -0.5 / (FF * C), None,
                                  ALU.mult).then_inc(pre_thr, 1)
                dve.wait_ge(pre_thr, 3 * n + 3)

            def masks(n, c):
                rows = slice(4 * c, 4 * c + 4) if n == 0 else slice(c, c + 1)
                w, pos, neg = (pre[name][:, rows] for name in (("wup", "up_pos", "up_neg"), ("wdn", "dn_pos", "dn_neg"))[n])
                dve.tensor_scalar(pos, w, thr[:, n:n + 1], None, ALU.is_gt).then_inc(masks_ready, 1)
                dve.tensor_scalar(neg, w, nthr[:, n:n + 1], None, ALU.is_lt).then_inc(masks_ready, 1)

            def ln_stats(g, pair):
                dve.wait_ge(x_loaded, 16 * g + 16)
                for i in range(2 * pair, 2 * pair + 2):
                    dve.bn_stats(stats[:, i], x_next[:, i]).then_inc(ln_step, 1)

            def ln_var(g):
                dve.wait_ge(ln_step, LN_STEPS * g + 4)
                dve.tensor_tensor(m_sum, stats[:, :, 1], stats[:, :, 4], ALU.add)
                dve.tensor_tensor(m_diff, stats[:, :, 1], stats[:, :, 4], ALU.subtract)
                dve.tensor_tensor(v_sum, stats[:, :, 2], stats[:, :, 5], ALU.add).then_inc(ln_step, 1)
                dve.wait_ge(ln_step, LN_STEPS * g + 5)
                dve.tensor_scalar(mean, m_sum, 0.5, None, ALU.mult)
                dve.scalar_tensor_tensor(out=m_diff, in0=m_diff, scalar=0.25, in1=m_diff,
                                         op0=ALU.mult, op1=ALU.mult).then_inc(ln_step, 1)
                dve.wait_ge(ln_step, LN_STEPS * g + 6)
                dve.scalar_tensor_tensor(out=var2[:, TILES:], in0=v_sum, scalar=1.0 / C, in1=m_diff,
                                         op0=ALU.mult, op1=ALU.add).then_inc(ln_step, 1)
                dve.wait_ge(ln_step, LN_STEPS * g + 7)
                dve.tensor_scalar(var2[:, 0:TILES], var2[:, TILES:], LN_EPS, None, ALU.add).then_inc(ln_in, 1)

            def ln_scale(g):
                dve.wait_ge(ln_roots, g + 1)
                dve.reciprocal(inv_sd, root[:, 0:TILES]).then_inc(ln_step, 1)
                dve.wait_ge(ln_step, LN_STEPS * g + 8)
                dve.tensor_tensor(rms, root[:, TILES:], inv_sd, ALU.mult).then_inc(ln_step, 1)
                dve.wait_ge(ln_step, LN_STEPS * g + 9)
                dve.tensor_scalar(rms, rms, RMS_EPS, None, ALU.add).then_inc(ln_step, 1)
                dve.wait_ge(ln_step, LN_STEPS * g + 10)
                dve.reciprocal(inv_rms, rms).then_inc(ln_step, 1)
                dve.wait_ge(ln_step, LN_STEPS * g + 11)
                dve.scalar_tensor_tensor(out=x_gain, in0=inv_sd, scalar=X_SCALE, in1=inv_rms,
                                         op0=ALU.mult, op1=ALU.mult).then_inc(x_gain_ready, 1)

            def proj_gains(g):
                dve.tensor_scalar(q_gain, rms, q_mul, None, ALU.mult)
                dve.tensor_scalar(k_gain, rms, w_unit, None, ALU.mult)
                dve.tensor_scalar(v_gain, rms, v_mul, None, ALU.mult).then_inc(gains_ready, 1)

            def normalise(g, i):
                if i == 0:
                    dve.wait_ge(x_gain_ready, g + 1)
                wait_if_any(dve, xlo_ready, 4 * g + max(i - 1, 0))
                dve.tensor_scalar(xf[:, i % 2], x_next[:, i], mean[:, i:i + 1], x_gain[:, i:i + 1],
                                  ALU.subtract, ALU.mult).then_inc(xf_ready, 1)

            def proj_to(dst, s, i, m, col, gain):
                n = 3 * i + m
                dve.wait_ge(proj_done, 12 * s + n + 1)
                dve.scalar_tensor_tensor(out=dst, in0=proj[n % 2][:], scalar=gain[:, i:i + 1],
                                         in1=bias[:, col], op0=ALU.mult, op1=ALU.add).then_inc(proj_out, 1)

            def k_first(s, i):
                if i == 0:
                    dve.wait_ge(gains_ready, s + 1)
                wait_if_any(dve, klo_ready, 4 * s + i)
                proj_to(kr.rearrange("p h d -> p (h d)"), s, i, 0, 1, k_gain)
                dve.wait_ge(proj_out, 12 * s + 3 * i + 1)
                dve.tensor_reduce(kmax[:], kr, AX.X, ALU.max).then_inc(kmax_ready, 1)
                dve.wait_ge(kmax_ready, 4 * s + i + 1)
                dve.tensor_tensor(kr, kr, kmax[:].unsqueeze(2).broadcast_to([P, HEADS, D]),
                                  ALU.subtract).then_inc(kd_ready, 1)

            def k_sum(s, i):
                dve.wait_ge(ke_ready, 4 * s + i + 1)
                wait_if_any(dve, kn_ready, 4 * s + i)
                dve.tensor_reduce(ksum[:], kr, AX.X, ALU.add).then_inc(ks_ready, 1)
                dve.wait_ge(ks_ready, 8 * s + 2 * i + 1)
                dve.tensor_scalar(ksum[:], ksum[:], 1.0 / K_SCALE, None, ALU.mult).then_inc(ks_ready, 1)
                dve.wait_ge(ks_ready, 8 * s + 2 * i + 2)
                dve.reciprocal(kinv[:], ksum[:]).then_inc(kinv_ready, 1)

            def q_first(s, i):
                wait_if_any(dve, qlo_ready, 4 * s + i)
                proj_to(qr.rearrange("p h d -> p (h d)"), s, i, 1, 0, q_gain)

            def v_first(s, i):
                wait_if_any(dve, vlo_ready, 4 * s + i)
                proj_to(vr, s, i, 2, 2, v_gain)
                dve.wait_ge(proj_out, 12 * s + 3 * i + 3)
                dve.transpose(v1, vr).then_inc(v1_ready, 1)
                dve.wait_ge(v1_ready, 4 * s + i + 1)
                dve.transpose(vr.rearrange("p (n a b) -> p n a b", n=OCT, b=2),
                              v1.rearrange("p (g n u) -> p n g u", g=HEADS, u=2)).then_inc(v2_ready, 1)

            def mask(s, i, j):
                n = 4 * i + j
                dve.wait_ge(sc_done, 16 * s + n + 1)
                wait_if_any(dve, alo_ready, 16 * s + max(n - 1, 0))
                dve.tensor_tensor(af[:, j % 2].rearrange("p (m n) -> p m n", m=4), sc[:],
                                  blocks[:].unsqueeze(1).broadcast_to([P, 4, P]),
                                  ALU.mult).then_inc(af_ready, 1)

            def h_parts(s, p):
                hp = hf[:, p % 2]
                dst = [hT[:, part, 2 * p:2 * p + 2].rearrange("p a b -> p (a b)") for part in range(2)]
                if p == 0:
                    wait_if_any(dve, down_done, 4 * s)
                dve.wait_ge(gelu_done, 16 * s + 2 * p + 2)
                dve.tensor_scalar(dst[0], hp, H_SCALE, None, ALU.mult).then_inc(hhi_ready, 1)
                dve.wait_ge(hhi_ready, 8 * s + p + 1)
                dve.scalar_tensor_tensor(out=dst[1], in0=hp, scalar=H_SCALE, in1=dst[0],
                                         op0=ALU.mult, op1=ALU.subtract).then_inc(hlo_ready, 1)

            def h_squares(s, p):
                dve.wait_ge(hsq_ready, 8 * s + p + 1)
                wait_if_any(dve, hacc_ready, 7 * s + (0 if p < 2 else max(p - 2, 1)))
                dve.tensor_tensor(hpart[:, p % 2], hsq[:, 0], hsq[:, 1], ALU.add).then_inc(hpart_ready, 1)

            def out_turn(s, i):
                dve.wait_ge(o0_ready, 8 * s + 2 * i + 2)
                dve.transpose(o1.rearrange("p (n d) -> p n d", n=OCT), o0[:, :, 0]).then_inc(o1_ready, 1)
                dve.wait_ge(o1_ready, 4 * s + i + 1)
                dve.transpose(o2.rearrange("p (h n u) -> p h n u", h=HEADS, u=2),
                              o1.rearrange("p (n h u) -> p h n u", h=HEADS, u=2)).then_inc(o2_ready, 1)

            def add_x(s, i):
                dve.wait_ge(res_ready, 4 * s + i + 1)
                dve.wait_ge(o2_ready, 4 * s + i + 1)
                dve.scalar_tensor_tensor(out=xres[:, i], in0=o2, scalar=o_unit, in1=xres[:, i],
                                         op0=ALU.mult, op1=ALU.add).then_inc(xo_ready, 1)

            def sum_squares(s):
                dve.wait_ge(ss_turned, s + 1)
                dve.tensor_reduce(h_sum, ud[1][:].rearrange("p (i f) -> p i f", i=TILES), AX.X,
                                  ALU.add).then_inc(ss_ready, 1)

            def h_gains(s):
                dve.wait_ge(ss_root, s + 1)
                dve.tensor_scalar(h_root, h_root, float(FF) ** -0.5, RMS_EPS, ALU.mult, ALU.add).then_inc(hg_step, 1)
                dve.wait_ge(hg_step, 3 * s + 1)
                dve.reciprocal(h_gain, h_root).then_inc(hg_step, 1)
                dve.wait_ge(hg_step, 3 * s + 2)
                dve.tensor_scalar(h_gain, h_gain, 1.0 / H_SCALE, None, ALU.mult).then_inc(hg_step, 1)
                dve.wait_ge(hg_step, 3 * s + 3)

            def final(s, i):
                dve.wait_ge(down_done, 4 * s + i + 1)
                dve.wait_ge(xo_ready, 4 * s + i + 1)
                dve.scalar_tensor_tensor(out=xres[:, i], in0=ud[i % 2][:], scalar=h_gain[:, i:i + 1],
                                         in1=xres[:, i], op0=ALU.mult, op1=ALU.add).then_inc(final_ready, 1)

            def group(s, more):
                for n in range(4):
                    def mask_quarter(j):
                        if n >= 2:
                            mask(s, n - 2, j)
                    k_first(s, n)
                    mask_quarter(0)
                    k_sum(s, n)
                    mask_quarter(1)
                    q_first(s, n)
                    h_parts(s, 2 * n)
                    mask_quarter(2)
                    h_squares(s, 2 * n)
                    v_first(s, n)
                    mask_quarter(3)
                    if n == 3:
                        out_turn(s, 0)
                    h_parts(s, 2 * n + 1)
                    h_squares(s, 2 * n + 1)
                mask(s, 2, 0)
                add_x(s, 0)
                mask(s, 2, 1)
                if more:
                    ln_stats(s + 1, 0)
                sum_squares(s)
                mask(s, 2, 2)
                if more:
                    ln_stats(s + 1, 1)
                mask(s, 2, 3)
                out_turn(s, 1)
                if more:
                    ln_var(s + 1)
                mask(s, 3, 0)
                h_gains(s)
                final(s, 0)
                mask(s, 3, 1)
                if more:
                    ln_scale(s + 1)
                    proj_gains(s + 1)
                    normalise(s + 1, 0)
                    normalise(s + 1, 1)
                mask(s, 3, 2)
                mask(s, 3, 3)
                add_x(s, 1)
                final(s, 1)
                if more:
                    normalise(s + 1, 2)
                out_turn(s, 2)
                add_x(s, 2)
                if more:
                    normalise(s + 1, 3)
                final(s, 2)
                out_turn(s, 3)
                add_x(s, 3)
                final(s, 3)

            own_token()
            ln_stats(0, 0)
            ln_stats(0, 1)
            ln_var(0)
            weight_max(0)
            ln_scale(0)
            normalise(0, 0)
            normalise(0, 1)
            weight_max(1)
            normalise(0, 2)
            weight_max(2)
            normalise(0, 3)
            weight_max(3)
            bias_max()
            prepare()
            proj_gains(0)
            up_sum(0)
            weight_lo(0)
            weight_lo(1)
            up_sum(2)
            weight_lo(2)
            weight_lo(3)
            threshold(0)
            for c in range(4):
                masks(0, c)
            threshold(1)
            for c in range(4):
                masks(1, c)
            dve.wait_ge(wt_turned, 16)
            group(0, True)
            with dve.Fori(1, GROUPS - 1) as s:
                group(s, True)
            group(GROUPS - 1, False)

        @block.scalar
        def _(act):
            def weight_sum(n, c):
                act.wait_ge((wup_in, wdn_in)[n][c], 16)
                if n == 0:
                    unread, w = pre["up_pos"][:, 4 * c:4 * c + 4], pre["wup"][:, 4 * c:4 * c + 4]
                else:
                    unread, w = pre["unread"][:, c % 3:c % 3 + 1], pre["wdn"][:, c:c + 1]
                    if c == 3:
                        act.wait_ge(dn_sum_done, 1)
                act.activation(unread.rearrange("p a b -> p (a b)"), w.rearrange("p a b -> p (a b)"), ACT.Abs,
                               accum_out=(up_sums, dn_sums)[n][:, c:c + 1]).then_inc((up_sum_done, dn_sum_done)[n], 1)

            def weight_hi(c):
                if c == 0:
                    act.wait_ge(w_gain_ready, 1)
                act.activation(wq16[:, 0, c], pre["wqkv"][:, c], ACT.Copy, scale=w_gain).then_inc(wq_hi_ready, 1)

            def weights_out(chunk):
                for n in range(4 * chunk, 4 * chunk + 4):
                    quarter = n % 4
                    act.wait_ge(wt_turned, n + 1)
                    bank = w_banks[n % 4]
                    if chunk < 4:
                        act.copy(wuT[:, quarter, chunk * 4 * P:(chunk + 1) * 4 * P], bank).then_inc(wt_out, 1)
                    else:
                        c = chunk - 4
                        act.copy(wdT[:, 4 * quarter:4 * quarter + 4, c * P:(c + 1) * P],
                                 bank.rearrange("p (m c) -> p m c", m=4)).then_inc(wt_out, 1)

            def x_hi(g, i):
                act.wait_ge(xf_ready, 4 * g + i + 1)
                wait_if_any(act, x_turned, 4 * g + max(i - 1, 0))
                act.copy(xs[:, i % 2, 0], xf[:, i % 2]).then_inc(xhi_ready, 1)

            def x_out(g, i):
                if i == 0:
                    wait_if_any(act, proj_done, 12 * g)
                    wait_if_any(act, up_done, 16 * g)
                act.wait_ge(x_turned, 4 * g + i + 1)
                act.copy(xT[:, :, :, i * P:(i + 1) * P],
                         tp[i % 2][:].rearrange("p (a c t) -> p a c t", a=2, c=CC)).then_inc(xT_ready, 1)

            def residual(s, i):
                if i == 0:
                    act.wait_ge(x_loaded, 16 * s + 16)
                    wait_if_any(act, stored, 64 * s)
                act.copy(xres[:, i], x_next[:, i]).then_inc(res_ready, 1)

            def qk_out(s, i, j):
                if j == 0:
                    wait_if_any(act, sc_done, 16 * s + 4 * max(i - 1, 0))
                act.wait_ge(qk_turned, 8 * s + 2 * i + j + 1)
                tiles = 2 * s + (i - 1) // 2 + 1
                wait_if_any(act, (kT_in, qT_in)[j][(i - 1) % 2], (64, 96)[j] * tiles)
                act.copy(rows[:, j].rearrange("p (x m t) -> p x m t", x=8, m=PAIRED),
                         tp[j][:].rearrange("p (m x t) -> p x m t", x=8, m=PAIRED)).then_inc(rows_out, 1)

            def gelu(s, f):
                p = f // 2
                wait_if_any(act, hlo_ready, 8 * s + max(p - 1, 0))
                act.wait_ge(up_done, 16 * s + f + 1)
                act.activation(hf[:, p % 2, (f % 2) * GT:(f % 2 + 1) * GT], ud[f % 2][:], ACT.Gelu,
                               scale=1.0 / X_SCALE).then_inc(gelu_done, 1)

            def square(s, p):
                act.wait_ge(gelu_done, 16 * s + 2 * p + 2)
                wait_if_any(act, hpart_ready, 8 * s + p)
                act.activation(hsq.rearrange("p a b -> p (a b)"), hf[:, p % 2], ACT.Square).then_inc(hsq_ready, 1)

            def q_hi(s, i):
                act.wait_ge(proj_out, 12 * s + 3 * i + 2)
                wait_if_any(act, qk_turned, 8 * s + 2 * i)
                act.copy(part16(Q16, 0), heads(qr)).then_inc(qhi_ready, 1)

            def k_exp(s, i):
                act.wait_ge(kd_ready, 4 * s + i + 1)
                act.activation(kr, kr, ACT.Exp).then_inc(ke_ready, 1)

            def k_hi(s, i):
                act.wait_ge(kn_ready, 4 * s + i + 1)
                wait_if_any(act, qk_turned, 8 * s + max(2 * i - 1, 0))
                act.copy(part16(K16, 0), heads(kr)).then_inc(khi_ready, 1)

            def v_hi(s, i):
                act.wait_ge(v2_ready, 4 * s + i + 1)
                wait_if_any(act, av_done, 16 * s)
                act.copy(V16[:, i, 0], vr).then_inc(vhi_ready, 1)

            def out_copy(s, i, h):
                act.wait_ge(av_done, 16 * s + 4 * i + 2 * h + 2)
                wait_if_any(act, o1_ready, 4 * s + i)
                act.copy(o0[:, 8 * h:8 * h + 8], ov[:]).then_inc(ov_out, 1)

            def att_hi(s, i, j):
                n = 4 * i + j
                act.wait_ge(af_ready, 16 * s + n + 1)
                wait_if_any(act, av_done, 16 * s + max(n - 3, 0))
                act.copy(a_hi[:, 4 * j:4 * j + 4].rearrange("p a b -> p (a b)"), af[:, j % 2]).then_inc(ahi_ready, 1)

            def group(s, more):
                for n in range(4):
                    def turned(j):
                        if n >= 1:
                            qk_out(s, n - 1, j)

                    def weights(j):
                        if n >= 2:
                            att_hi(s, n - 2, j)
                    turned(0)
                    if n == 3:
                        out_copy(s, 0, 0)
                    k_exp(s, n)
                    weights(0)
                    gelu(s, 4 * n)
                    turned(1)
                    weights(1)
                    k_hi(s, n)
                    gelu(s, 4 * n + 1)
                    if n == 3:
                        out_copy(s, 0, 1)
                    square(s, 2 * n)
                    q_hi(s, n)
                    if n < 2:
                        residual(s, 2 * n)
                        residual(s, 2 * n + 1)
                    weights(2)
                    gelu(s, 4 * n + 2)
                    v_hi(s, n)
                    weights(3)
                    gelu(s, 4 * n + 3)
                    square(s, 2 * n + 1)
                qk_out(s, 3, 0)
                out_copy(s, 1, 0)
                qk_out(s, 3, 1)
                att_hi(s, 2, 0)
                att_hi(s, 2, 1)
                out_copy(s, 1, 1)
                att_hi(s, 2, 2)
                att_hi(s, 2, 3)
                att_hi(s, 3, 0)
                out_copy(s, 2, 0)
                att_hi(s, 3, 1)
                if more:
                    x_hi(s + 1, 0)
                    x_hi(s + 1, 1)
                att_hi(s, 3, 2)
                att_hi(s, 3, 3)
                out_copy(s, 2, 1)
                if more:
                    x_out(s + 1, 0)
                    x_hi(s + 1, 2)
                out_copy(s, 3, 0)
                if more:
                    x_out(s + 1, 1)
                    x_hi(s + 1, 3)
                out_copy(s, 3, 1)
                if more:
                    x_out(s + 1, 2)
                    x_out(s + 1, 3)

            x_hi(0, 0)
            x_hi(0, 1)
            x_out(0, 0)
            x_hi(0, 2)
            x_out(0, 1)
            x_hi(0, 3)
            x_out(0, 2)
            x_out(0, 3)
            weight_hi(0)
            weight_hi(1)
            weight_sum(0, 1)
            weight_hi(2)
            weight_sum(0, 3)
            weight_hi(3)
            weight_sum(1, 0)
            weight_sum(1, 1)
            weight_sum(1, 2)
            weights_out(0)
            weight_sum(1, 3)
            weights_out(1)
            weights_out(2)
            weights_out(3)
            for c in range(4):
                weights_out(4 + c)
            act.wait_ge(wq_lo_ready, CC)
            group(0, True)
            with act.Fori(1, GROUPS - 1) as s:
                group(s, True)
            group(GROUPS - 1, False)

        @block.gpsimd
        def _(pool):
            def prepare():
                pool.memset(ident32[:], 1.0).then_inc(consts_step, 1)
                pool.memset(ident[:], 1.0).then_inc(consts_step, 1)
                pool.memset(order[:], 1.0).then_inc(consts_step, 1)
                pool.memset(minus_ident[:], -1.0).then_inc(consts_step, 1)
                pool.memset(blocks[:], 1.0 / K_SCALE).then_inc(consts_step, 1)
                pool.memset(half[:], 0.5).then_inc(consts_made, 1)
                pool.wait_ge(consts_step, 5)
                pool.affine_select(out=ident32[:], in_=ident32[:], compare_op=ALU.is_equal, fill=0.0, base=0,
                                   pattern=[[-1, P]], channel_multiplier=1).then_inc(consts_made, 1)
                pool.affine_select(out=ident[:], in_=ident[:], compare_op=ALU.is_equal, fill=0.0, base=0,
                                   pattern=[[-1, P]], channel_multiplier=1).then_inc(consts_made, 1)
                pool.affine_select(out=minus_ident[:], in_=minus_ident[:], compare_op=ALU.is_equal, fill=0.0, base=0,
                                   pattern=[[-1, P]], channel_multiplier=1).then_inc(consts_made, 1)
                for i in range(2):
                    o3 = order[:, 64 * i:64 * i + 64].rearrange("p (q u l) -> p q u l", q=4, u=2)
                    pool.affine_select(out=o3, in_=o3, compare_op=ALU.is_equal, fill=0.0, base=-16 * i,
                                       pattern=[[-32, 4], [-1, 2], [-2, 8]],
                                       channel_multiplier=1).then_inc(consts_made, 1)
                b3 = blocks[:].rearrange("p (a b) -> p a b", b=32)
                pool.affine_select(out=b3, in_=b3, compare_op=ALU.is_ge, fill=0.0, base=0,
                                   pattern=[[-32, 4], [0, 32]], channel_multiplier=1).then_inc(consts_step, 1)
                pool.wait_ge(consts_step, 6)
                pool.affine_select(out=b3, in_=b3, compare_op=ALU.is_ge, fill=0.0, base=31,
                                   pattern=[[32, 4], [0, 32]],
                                   channel_multiplier=-1).then_inc(consts_made, 1)

            def all_reduce(first, last, producer, value, op):
                pool.wait_ge(producer, value)
                pool.partition_all_reduce(g_parts[:, first:last], parts[:, first:last], P, op).then_inc(abs_all, 1)

            def ln_pow(g):
                pool.wait_ge(ln_in, g + 1)
                pool.tensor_tensor(root[:], var2[:], half[:], ALU.pow).then_inc(ln_roots, 1)

            def h_pow(s):
                pool.wait_ge(ss_ready, s + 1)
                pool.tensor_tensor(h_root, h_sum, half[:, 0:TILES], ALU.pow).then_inc(ss_root, 1)

            def x_lo(g, i):
                pool.wait_ge(xhi_ready, 4 * g + i + 1)
                pool.tensor_tensor(xs[:, i % 2, 1], xf[:, i % 2], xs[:, i % 2, 0],
                                   ALU.subtract).then_inc(xlo_ready, 1)

            def q_lo(s, i):
                pool.wait_ge(qhi_ready, 4 * s + i + 1)
                pool.tensor_tensor(part16(Q16, 1), heads(qr), part16(Q16, 0), ALU.subtract).then_inc(qlo_ready, 1)

            def k_norm(s, i):
                pool.wait_ge(kinv_ready, 4 * s + i + 1)
                pool.tensor_tensor(kr, kr, kinv[:].unsqueeze(2).broadcast_to([P, HEADS, D]),
                                   ALU.mult).then_inc(kn_ready, 1)

            def k_lo(s, i):
                pool.wait_ge(khi_ready, 4 * s + i + 1)
                pool.tensor_tensor(part16(K16, 1), heads(kr), part16(K16, 0), ALU.subtract).then_inc(klo_ready, 1)

            def v_lo(s, i):
                pool.wait_ge(vhi_ready, 4 * s + i + 1)
                pool.tensor_tensor(V16[:, i, 1], vr, V16[:, i, 0], ALU.subtract).then_inc(vlo_ready, 1)

            def out_add(s, i, h):
                pool.wait_ge(ov_out, 8 * s + 2 * i + h + 1)
                half_tile = o0[:, 8 * h:8 * h + 8]
                pool.tensor_tensor(half_tile[:, :, 0], half_tile[:, :, 0], half_tile[:, :, 1],
                                   ALU.add).then_inc(o0_ready, 1)

            def att_lo(s, i, j):
                pool.wait_ge(ahi_ready, 16 * s + 4 * i + j + 1)
                pool.tensor_tensor(a_lo[:, 4 * j:4 * j + 4].rearrange("p a b -> p (a b)"), af[:, j % 2],
                                   a_hi[:, 4 * j:4 * j + 4].rearrange("p a b -> p (a b)"),
                                   ALU.subtract).then_inc(alo_ready, 1)

            def h_add(s, p):
                if p == 1:
                    wait_if_any(pool, ss_turned, s)
                else:
                    pool.wait_ge(hacc_ready, 7 * s + p - 1)
                pool.wait_ge(hpart_ready, 8 * s + p + 1)
                pool.tensor_tensor(hacc, hpart[:, 0] if p == 1 else hacc, hpart[:, p % 2],
                                   ALU.add).then_inc(hacc_ready, 1)

            def group(s, more):
                for n in range(4):
                    def weights(j):
                        if n >= 2:
                            att_lo(s, n - 2, j)
                    if n:
                        h_add(s, 2 * n - 1)
                    weights(0)
                    k_norm(s, n)
                    if n == 3:
                        out_add(s, 0, 0)
                    weights(1)
                    k_lo(s, n)
                    if n:
                        h_add(s, 2 * n)
                    if n == 3:
                        out_add(s, 0, 1)
                    q_lo(s, n)
                    weights(2)
                    v_lo(s, n)
                    weights(3)
                h_add(s, 7)
                out_add(s, 1, 0)
                att_lo(s, 2, 0)
                att_lo(s, 2, 1)
                out_add(s, 1, 1)
                att_lo(s, 2, 2)
                h_pow(s)
                att_lo(s, 2, 3)
                if more:
                    ln_pow(s + 1)
                att_lo(s, 3, 0)
                out_add(s, 2, 0)
                att_lo(s, 3, 1)
                if more:
                    x_lo(s + 1, 0)
                    x_lo(s + 1, 1)
                att_lo(s, 3, 2)
                att_lo(s, 3, 3)
                out_add(s, 2, 1)
                if more:
                    x_lo(s + 1, 2)
                out_add(s, 3, 0)
                if more:
                    x_lo(s + 1, 3)
                out_add(s, 3, 1)

            prepare()
            ln_pow(0)
            for i in range(TILES):
                x_lo(0, i)
            all_reduce(0, 5, max_done, 5, bass.bass_isa.ReduceOp.max)
            all_reduce(5, 9, up_sum_done, 4, bass.bass_isa.ReduceOp.add)
            all_reduce(9, 13, dn_sum_done, 4, bass.bass_isa.ReduceOp.add)
            pool.wait_ge(wt_turned, 32)
            pool.wait_ge(wq_lo_ready, CC)
            group(0, True)
            with pool.Fori(1, GROUPS - 1) as s:
                group(s, True)
            group(GROUPS - 1, False)


_INS = ['L0_attn_x', 'L0_attn_W_qkv', 'L0_attn_b_qkv', 'L0_ffn_w_up', 'L0_ffn_w_down']
_OUTS = [((8, 1024, 512), 'float32')]


def kernel(**inputs):
    import numpy as _np
    import concourse.bacc as _bacc
    from concourse import mybir as _mybir
    from concourse.bass_utils import run_bass_kernel_spmd as _run

    nc = _bacc.Bacc("TRN2", target_bir_lowering=False, num_devices=1)
    arrays, args = {}, []
    for name in _INS:
        a = _np.ascontiguousarray(inputs[name])
        arrays[f"in_{name}_dram"] = a
        args.append(nc.dram_tensor(f"in_{name}_dram", a.shape, _mybir.dt.from_np(a.dtype), kind="ExternalInput").ap())
    for i, (shape, dtype) in enumerate(_OUTS):
        dt = _mybir.dt.from_np(_np.dtype(dtype))
        args.append(nc.dram_tensor(f"out_{i}_dram", shape, dt, kind="ExternalOutput").ap())
    layer_kernel(nc, *args)
    r = _run(nc, [arrays], core_ids=[0])
    return r.results[0]["out_0_dram"]
```
